# Optimizing a Trainium2 kernel written in Bass

```python
import numpy as np
import jax
import jax.numpy as jnp

def _softmax(x, axis=-1):
    return jax.nn.softmax(x, axis=axis)

def _gelu(x):
    return jax.nn.gelu(x, approximate=True)

def _silu(x):
    return jax.nn.silu(x)

def _sigmoid(x):
    return jax.nn.sigmoid(x)

def _layernorm(x, axis=-1, eps=1e-05):
    m = jnp.mean(x, axis=axis, keepdims=True)
    v = jnp.var(x, axis=axis, keepdims=True)
    return (x - m) / jnp.sqrt(v + eps)

def _scatter_add(tgt, idx, src, axis=0):
    return tgt.at[idx].add(src)

def _segment_sum(src, seg, n):
    return jax.ops.segment_sum(src, seg, n)
kernel_name = 'mk_xattn_seq_d1_seqx_r4_36b155'

def setup_inputs(seed: int=0):
    np.random.seed(seed)
    _w = jnp.asarray

    def _rec_inputs():
        import jax
        import jax.numpy as jnp
        _rk = jax.random.key(seed)
        x = 7.22e-05 + 1 * jax.random.normal(jax.random.fold_in(_rk, 1), (1, 2048, 256), jnp.float32)
        _lenS = 2048 - jax.random.randint(jax.random.fold_in(_rk, 7), (1,), 0, max(1, 2048 // 4) + 1, jnp.int32)
        _lenS2 = 1601 - jax.random.randint(jax.random.fold_in(_rk, 8), (1,), 0, max(1, 1601 // 4) + 1, jnp.int32)
        _ctx_768P = jax.random.normal(jax.random.fold_in(_rk, 11), (1, 16, 192), jnp.float32)
        _ctx_768c = jax.random.dirichlet(jax.random.fold_in(_rk, 511), 0.3 * jnp.ones((16,), jnp.float32), (1, 1601))
        _ctx_768t = jnp.einsum('bsk,bkd->bsd', _ctx_768c, _ctx_768P)
        _ctx_768t = _ctx_768t * jax.lax.rsqrt(jnp.mean(jnp.square(_ctx_768t)) + 1e-12) * 0.953939
        ctx_768 = 0.000651243 + 0.998673 * (_ctx_768t + 0.3 * jax.random.normal(jax.random.fold_in(_rk, 611), (1, 1601, 192), jnp.float32))
        return (x, ctx_768)
    x, ctx_768 = _rec_inputs()

    def _L0_xattn_setup():
        import jax, jax.numpy as jnp
        import numpy as np
        HEADS = 16
        D_HEAD = 64
        EPS = 1e-05

        def _ln(x, g, b):
            m = jnp.mean(x, axis=-1, keepdims=True)
            v = jnp.var(x, axis=-1, keepdims=True)
            return (x - m) * jax.lax.rsqrt(v + EPS) * g + b

        def _attn(xq, xc, Wq, Wk, Wv, Wo, bo):
            B, N, _ = xq.shape
            S = xc.shape[1]
            q = (xq @ Wq).reshape(B, N, HEADS, D_HEAD)
            k = (xc @ Wk).reshape(B, S, HEADS, D_HEAD)
            v = (xc @ Wv).reshape(B, S, HEADS, D_HEAD)
            scale = D_HEAD ** (-0.5)
            scores = jnp.einsum('bnhd,bshd->bhns', q, k) * scale
            attn = jax.nn.softmax(scores, axis=-1)
            out = jnp.einsum('bhns,bshd->bnhd', attn, v).reshape(B, N, HEADS * D_HEAD)
            return out @ Wo + bo

        def _geglu_ff(x, Wp, bp, Wf, bf):
            h = x @ Wp + bp
            a, gate = jnp.split(h, 2, axis=-1)
            return a * jax.nn.gelu(gate, approximate=False) @ Wf + bf
        key = jax.random.key(seed)
        ks = jax.random.split(key, 16)
        dim, ctx, inner, ffin = (256, 192, HEADS * D_HEAD, 4 * 256)

        def w(k, i, o):
            return jax.random.normal(k, (i, o), jnp.float32) * i ** (-0.5)
        inp = {'x': jax.random.normal(ks[0], (4, 512, dim), jnp.float32), 'context': jax.random.normal(ks[1], (4, 77, ctx), jnp.float32), 'Wq1': w(ks[2], dim, inner), 'Wk1': w(ks[3], dim, inner), 'Wv1': w(ks[4], dim, inner), 'Wo1': w(ks[5], inner, dim), 'bo1': jnp.zeros((dim,), jnp.float32), 'Wq2': w(ks[6], dim, inner), 'Wk2': w(ks[7], ctx, inner), 'Wv2': w(ks[8], ctx, inner), 'Wo2': w(ks[9], inner, dim), 'bo2': jnp.zeros((dim,), jnp.float32), 'Wp': w(ks[10], dim, 2 * ffin), 'bp': jnp.zeros((2 * ffin,), jnp.float32), 'Wf': w(ks[11], ffin, dim), 'bf': jnp.zeros((dim,), jnp.float32), 'g1': jnp.ones((dim,), jnp.float32), 'b1': jnp.zeros((dim,), jnp.float32), 'g2': jnp.ones((dim,), jnp.float32), 'b2': jnp.zeros((dim,), jnp.float32), 'g3': jnp.ones((dim,), jnp.float32), 'b3': jnp.zeros((dim,), jnp.float32)}
        return inp
    _L0_xattn_all = _L0_xattn_setup()
    _L0_xattn_in = {k: v for k, v in _L0_xattn_all.items() if k in ('Wq1', 'Wk1', 'Wv1', 'Wo1', 'bo1', 'Wq2', 'Wk2', 'Wv2', 'Wo2', 'bo2', 'Wp', 'bp', 'Wf', 'bf', 'g1', 'b1', 'g2', 'b2', 'g3', 'b3')}
    del _L0_xattn_all
    return {'x': x, 'ctx_768': ctx_768, 'L0_xattn_Wq1': _L0_xattn_in['Wq1'], 'L0_xattn_Wk1': _L0_xattn_in['Wk1'], 'L0_xattn_Wv1': _L0_xattn_in['Wv1'], 'L0_xattn_Wo1': _L0_xattn_in['Wo1'], 'L0_xattn_bo1': _L0_xattn_in['bo1'], 'L0_xattn_Wq2': _L0_xattn_in['Wq2'], 'L0_xattn_Wk2': _L0_xattn_in['Wk2'], 'L0_xattn_Wv2': _L0_xattn_in['Wv2'], 'L0_xattn_Wo2': _L0_xattn_in['Wo2'], 'L0_xattn_bo2': _L0_xattn_in['bo2'], 'L0_xattn_Wp': _L0_xattn_in['Wp'], 'L0_xattn_bp': _L0_xattn_in['bp'], 'L0_xattn_Wf': _L0_xattn_in['Wf'], 'L0_xattn_bf': _L0_xattn_in['bf'], 'L0_xattn_g1': _L0_xattn_in['g1'], 'L0_xattn_b1': _L0_xattn_in['b1'], 'L0_xattn_g2': _L0_xattn_in['g2'], 'L0_xattn_b2': _L0_xattn_in['b2'], 'L0_xattn_g3': _L0_xattn_in['g3'], 'L0_xattn_b3': _L0_xattn_in['b3']}

def reference(x, ctx_768, L0_xattn_Wq1, L0_xattn_Wk1, L0_xattn_Wv1, L0_xattn_Wo1, L0_xattn_bo1, L0_xattn_Wq2, L0_xattn_Wk2, L0_xattn_Wv2, L0_xattn_Wo2, L0_xattn_bo2, L0_xattn_Wp, L0_xattn_bp, L0_xattn_Wf, L0_xattn_bf, L0_xattn_g1, L0_xattn_b1, L0_xattn_g2, L0_xattn_b2, L0_xattn_g3, L0_xattn_b3):
    import jax
    import jax.numpy as jnp

    def _L0_xattn_ref(x, context, Wq1, Wk1, Wv1, Wo1, bo1, Wq2, Wk2, Wv2, Wo2, bo2, Wp, bp, Wf, bf, g1, b1, g2, b2, g3, b3):
        import jax, jax.numpy as jnp
        import numpy as np
        HEADS = 16
        D_HEAD = 64
        EPS = 1e-05

        def _ln(x, g, b):
            m = jnp.mean(x, axis=-1, keepdims=True)
            v = jnp.var(x, axis=-1, keepdims=True)
            return (x - m) * jax.lax.rsqrt(v + EPS) * g + b

        def _attn(xq, xc, Wq, Wk, Wv, Wo, bo):
            B, N, _ = xq.shape
            S = xc.shape[1]
            q = (xq @ Wq).reshape(B, N, HEADS, D_HEAD)
            k = (xc @ Wk).reshape(B, S, HEADS, D_HEAD)
            v = (xc @ Wv).reshape(B, S, HEADS, D_HEAD)
            scale = D_HEAD ** (-0.5)
            scores = jnp.einsum('bnhd,bshd->bhns', q, k) * scale
            attn = jax.nn.softmax(scores, axis=-1)
            out = jnp.einsum('bhns,bshd->bnhd', attn, v).reshape(B, N, HEADS * D_HEAD)
            return out @ Wo + bo

        def _geglu_ff(x, Wp, bp, Wf, bf):
            h = x @ Wp + bp
            a, gate = jnp.split(h, 2, axis=-1)
            return a * jax.nn.gelu(gate, approximate=False) @ Wf + bf
        x = _attn(_ln(x, g1, b1), _ln(x, g1, b1), Wq1, Wk1, Wv1, Wo1, bo1) + x
        x = _attn(_ln(x, g2, b2), context, Wq2, Wk2, Wv2, Wo2, bo2) + x
        x = _geglu_ff(_ln(x, g3, b3), Wp, bp, Wf, bf) + x
        return x
    x = _L0_xattn_ref(x, ctx_768, L0_xattn_Wq1, L0_xattn_Wk1, L0_xattn_Wv1, L0_xattn_Wo1, L0_xattn_bo1, L0_xattn_Wq2, L0_xattn_Wk2, L0_xattn_Wv2, L0_xattn_Wo2, L0_xattn_bo2, L0_xattn_Wp, L0_xattn_bp, L0_xattn_Wf, L0_xattn_bf, L0_xattn_g1, L0_xattn_b1, L0_xattn_g2, L0_xattn_b2, L0_xattn_g3, L0_xattn_b3)
    return x

_drawn_inputs = setup_inputs


def setup_inputs(seed=0):
    import zlib

    import numpy as np

    out = dict(_drawn_inputs(seed))
    spreads = {'L0_xattn_bo1': (0.0, 0.1),
     'L0_xattn_bo2': (0.0, 0.1),
     'L0_xattn_bp': (0.0, 0.1),
     'L0_xattn_bf': (0.0, 0.1),
     'L0_xattn_g1': (1.0, 0.2),
     'L0_xattn_b1': (0.0, 0.1),
     'L0_xattn_g2': (1.0, 0.2),
     'L0_xattn_b2': (0.0, 0.461),
     'L0_xattn_g3': (1.0, 0.2),
     'L0_xattn_b3': (0.0, 0.1)}
    factors = {}
    for name, (base, spread) in spreads.items():
        noise = np.random.default_rng([zlib.crc32(name.encode()), seed]).standard_normal(out[name].shape)
        drawn = base * np.exp(spread * noise) if base else spread * noise
        out[name] = jnp.asarray(drawn.astype(out[name].dtype))
    for name, factor in factors.items():
        out[name] = (out[name] * factor).astype(out[name].dtype)
    return out
```

```python
from contextlib import ExitStack

import concourse.bass as bass
from concourse import mybir

FP32 = mybir.dt.float32
FP32R = mybir.dt.float32r
ALU = mybir.AluOpType
ACT = mybir.ActivationFunctionType
AX = mybir.AxisListType

P = 128
HALF = P // 2
BANK = 512
TOKENS, DIM, CTX_TOKENS, CTX_DIM = 2048, 256, 1601, 192
HEADS, HEAD_DIM = 16, 64
INNER = HEADS * HEAD_DIM
FF = 1024
EPS = 1e-5
SCALE = HEAD_DIM ** -0.5
DIM_TILES = DIM // P
TOKEN_TILES = TOKENS // P
CHUNKS = TOKENS // BANK
PAIRS = HEADS // 2
UNITS = PAIRS * CHUNKS
PERIOD = 2 * CHUNKS
Q_TILES = BANK // P
MAX_TILES = 2 * Q_TILES * 4
RING = 4
CTX_TILES = -(-CTX_TOKENS // P)
CTX_LAST = CTX_TOKENS - (CTX_TILES - 1) * P
FF_TILES = FF // P


class Unit:

    def __init__(self, u, i=None):
        self.u, self.i = u, i
        self.chunk = u % CHUNKS
        self.parity = u % 2
        self.pair_parity = (u // CHUNKS) % 2
        self.first = u == 0 and i is None
        self.has_next = i is not None or u < UNITS - 1
        self.has_next_pair = i is not None or u < UNITS - CHUNKS

    def at(self, value, per_period):
        return value if self.i is None else self.i * per_period + value


def units(eng):
    yield Unit(0)
    loops = (UNITS - 1) // PERIOD
    with eng.Fori(0, loops) as i:
        for u in range(1, PERIOD + 1):
            yield Unit(u, i)
    for u in range(1 + loops * PERIOD, UNITS):
        yield Unit(u)


class Attention:

    def __init__(self, name, keys, key_chunks, max_chunks, key_rows, slots, max_steps, dve_adds):
        self.name, self.keys = name, keys
        self.steps = -(-keys // P)
        self.tile_keys = [min(P, keys - t * P) for t in range(self.steps)]
        self.key_chunks = key_chunks
        self.max_chunks = max_chunks
        self.key_rows = key_rows
        self.slots = slots
        assert sum(max_steps) == MAX_TILES and len(max_steps) == self.steps
        self.max_at = [list(range(sum(max_steps[:t]), sum(max_steps[:t + 1]))) for t in range(self.steps)]
        self.dve_adds = dve_adds
        taken = [s for group in dve_adds for s in group]
        rest = [s for s in range(self.steps) if s not in taken]
        self.pool_adds = [tuple(rest[:2])] + [(s,) for s in rest[2:]]
        self.number, n = {}, 0
        for name in ["k0", "k1", "k2", "k3", "q", "v0", "v1", "v2", "v3", "row0", "row1"]:
            self.number[-1, name] = n
            n += 1
        for u in range(UNITS):
            for t in range(self.steps):
                for name in self.jobs_at(Unit(u), t):
                    self.number[u, name] = n
                    n += 1
        for name in ("sum", "y0", "y1"):
            self.number[UNITS, name] = n
            n += 1
        self.period_jobs = self.number[PERIOD + 1, "q"] - self.number[1, "q"]
        self.all_jobs = n

    def jobs_at(self, unit, t):
        names = []
        for slot, name in self.slots:
            if slot == t:
                if name in ("q", "row0", "row1") and not unit.has_next:
                    continue
                if name in ("kv0", "kv1"):
                    if not unit.has_next_pair:
                        continue
                    which = 2 * (unit.chunk % 2) + int(name[2])
                    name = ("k" if unit.chunk < 2 else "v") + str(which)
                if name in ("sum", "y0", "y1") and unit.first:
                    continue
                names.append(name)
        return names

    def job(self, unit, name):
        return unit.at(self.number[unit.u, name], self.period_jobs)

    def step(self, unit, t):
        return unit.at(unit.u * self.steps + t, PERIOD * self.steps)

    def adder(self, unit, t):
        back = 0 if t >= 0 else 1
        s = t + back * self.steps
        for kind, adds in (("dve", self.dve_adds), ("pool", self.pool_adds)):
            for n, group in enumerate(adds):
                if s in group:
                    return kind, unit.at((unit.u - back) * len(adds) + n + 1, PERIOD * len(adds))


def wait(eng, sem, value):
    if not isinstance(value, int) or value > 0:
        eng.wait_ge(sem, value)


def xattn_block(nc, x, ctx_768, Wq1, Wk1, Wv1, Wo1, bo1, Wq2, Wk2, Wv2, Wo2, bo2, Wp, bp, Wf, bf,
                g1, b1, g2, b2, g3, b3, out):
    self_attn = Attention(
        "self", TOKENS, [(BANK * j, BANK) for j in range(4)], [(BANK * j, BANK) for j in range(4)], [P, P],
        [(0, "q"), (2, "kv0"), (4, "sum"), (9, "y0"), (10, "y1"), (11, "row0"), (13, "row1"), (14, "kv1")],
        [0, 0, 2, 3, 3, 3, 3, 3, 3, 3, 3, 3, 3, 0, 0, 0], [(0, 1), (12,), (14,)])
    width = -(-CTX_TOKENS // 8) * 2
    cross_attn = Attention(
        "cross", CTX_TOKENS, [(BANK * j, min(BANK, CTX_TOKENS - BANK * j)) for j in range(4)],
        [(min(j * (width - 2), CTX_TOKENS - width), width) for j in range(4)], [P, CTX_DIM - P],
        [(0, "q"), (2, "kv0"), (4, "sum"), (8, "y0"), (9, "y1"), (10, "row0"), (11, "row1"), (12, "kv1")],
        [0, 0, 2, 3, 3, 3, 4, 4, 4, 4, 4, 1, 0], [(0, 1), (10,)])
    assert cross_attn.max_chunks[-1][0] + width == CTX_TOKENS
    layers = [self_attn, cross_attn]

    x_dram = x.rearrange("b (t p) d -> p (b t) d", p=P)
    out_dram = out.rearrange("b (t p) d -> p (b t) d", p=P)
    ctx_rows = ctx_768.rearrange("b t d -> (b t) d")
    wq_dram = [w.rearrange("(c p) n -> p c n", p=P) for w in (Wq1, Wq2)]
    wo_dram = [w.rearrange("(r p) n -> p r n", p=P) for w in (Wo1, Wo2)]

    ctx = ExitStack()
    with ctx:
        def sb(name, shape, dtype=FP32, stack=ctx):
            return stack.enter_context(nc.sbuf_tensor(name, shape, dtype))

        def sem(name):
            return ctx.enter_context(nc.semaphore(name))

        x_sb = sb("x_sb", [P, TOKEN_TILES, DIM])
        xn_t = sb("xn_t", [P, DIM_TILES, TOKENS])
        ctx_t = sb("ctx_t", [P, 2, CTX_TOKENS])
        q_hi = [[sb(f"q_hi{b}{a}", [P, BANK], FP32R) for a in range(2)] for b in range(2)]
        q_lo = [[sb(f"q_lo{b}{a}", [HALF + 1, BANK], FP32R) for a in range(2)] for b in range(2)]
        v_sb = sb("v_sb", [P, 2, TOKEN_TILES, P])
        probs = sb("probs", [P, RING, 2, BANK])
        pool_sum = sb("pool_sum", [P, 2, BANK])
        dve_sum = sb("dve_sum", [P, 2, 2, BANK])
        w_q = [[sb(f"w_q{l}{b}", [P, DIM_TILES, P]) for b in range(2)] for l in range(2)]
        w_k = [[sb(f"w_k{l}{b}", [P, DIM_TILES, P]) for b in range(2)] for l in range(2)]
        w_v = [[sb(f"w_v{l}{b}", [P, DIM_TILES, P]) for b in range(2)] for l in range(2)]
        w_o = [[sb(f"w_o{l}{b}", [P, DIM]) for b in range(2)] for l in range(2)]
        o_raw = sb("o_raw", [P, 2, BANK])
        o_norm = sb("o_norm", [P, BANK])
        sum_recip = sb("sum_recip", [P, BANK])
        part_max = sb("part_max", [P, 2 * Q_TILES, 4])
        query_max = sb("query_max", [P, 2 * Q_TILES])
        max_rows = [sb(f"max_rows{a}", [Q_TILES, P], FP32R) for a in range(2)]
        ident = sb("ident", [P, P])
        ones = sb("ones", [P, P])
        one_row = sb("one_row", [1, BANK])
        eps_col = sb("eps_col", [P, 1])
        gains = sb("gains", [P, 3, DIM_TILES])
        shifts = sb("shifts", [P, 3, DIM_TILES])
        bias_b = sb("bias_b", [P, 3, DIM])
        bp_sb = sb("bp_sb", [P, 2 * FF_TILES])
        stats = sb("stats", [P, TOKEN_TILES, 6])
        moments = sb("moments", [P, TOKEN_TILES, 2])
        std = sb("std", [P, TOKEN_TILES])
        rstd = sb("rstd", [P, TOKEN_TILES])
        attn_memory = ExitStack()
        k_hi_lo = [[sb(f"k_hi_lo{b}{a}", [P, TOKENS], FP32R, attn_memory) for a in range(2)] for b in range(2)]
        k_hi_one = [[sb(f"k_hi_one{b}{a}", [HALF + 1, TOKENS], FP32R, attn_memory) for a in range(2)]
                    for b in range(2)]
        attn_memory.close()
        w_p = sb("w_p", [P, DIM_TILES, 2 * FF])
        w_f = sb("w_f", [P, FF_TILES, DIM])
        gelu_sb = sb("gelu_sb", [P, 2, BANK])
        hidden = sb("hidden", [P, FF_TILES, BANK])

        xn_stage = probs[:, :, :, :].rearrange("p r a n -> p (r a n)").rearrange("p (t d) -> p t d", d=DIM)
        ctx_stage = v_sb[:, :, :, :].rearrange("p b t n -> p (b t n)")[:, 0:CTX_TILES * CTX_DIM].rearrange(
            "p (t d) -> p t d", d=CTX_DIM)

        def bank(name):
            return ctx.enter_context(nc.psum_tensor(name, [P, BANK], FP32))

        score_banks = [bank(f"scores{n}") for n in range(2)]
        max_banks = [bank(f"max_scores{n}") for n in range(4)]
        out_bank = bank("attn_out")
        work_bank = bank("work")
        four_banks = [work_bank, out_bank] + score_banks

        x_loaded = [sem(f"x_loaded{g}") for g in range(4)]
        ctx_loaded = sem("ctx_loaded")
        vec_loaded = sem("vec_loaded")
        ff_loaded = sem("ff_loaded")
        qkv_loaded = [[sem(f"qkv_loaded{l}{b}") for b in range(2)] for l in range(2)]
        wo_loaded = [[sem(f"wo_loaded{l}{b}") for b in range(2)] for l in range(2)]
        consts_set = sem("consts_set")
        ident_zeroed = sem("ident_zeroed")
        ident_ready = sem("ident_ready")
        key_ones = sem("key_ones")
        stats_done = sem("stats_done")
        moments_done = sem("moments_done")
        std_done = sem("std_done")
        rstd_done = sem("rstd_done")
        normalised = sem("normalised")
        xn_turned = sem("xn_turned")
        xn_ready = sem("xn_ready")
        ctx_turned = sem("ctx_turned")
        ctx_ready = sem("ctx_ready")
        bias_added = sem("bias_added")
        scores_ready = [sem(f"scores_ready{l}") for l in range(2)]
        probs_ready = [sem(f"probs_ready{l}") for l in range(2)]
        values_used = [sem(f"values_used{l}") for l in range(2)]
        max_tile_ready = [sem(f"max_tile_ready{l}") for l in range(2)]
        max_tile_taken = [sem(f"max_tile_taken{l}") for l in range(2)]
        head_max_ready = [sem(f"head_max_ready{l}") for l in range(2)]
        work_ready = [sem(f"work_ready{l}") for l in range(2)]
        work_taken = [sem(f"work_taken{l}") for l in range(2)]
        queries_doubled = [sem(f"queries_doubled{l}") for l in range(2)]
        keys_doubled = [sem(f"keys_doubled{l}") for l in range(2)]
        rows_placed = [[sem(f"rows_placed{l}{a}") for a in range(2)] for l in range(2)]
        hi_ready = [sem(f"hi_ready{l}") for l in range(2)]
        pool_added = [sem(f"pool_added{l}") for l in range(2)]
        dve_added = [sem(f"dve_added{l}") for l in range(2)]
        sums_merged = [sem(f"sums_merged{l}") for l in range(2)]
        out_copied = [sem(f"out_copied{l}") for l in range(2)]
        out_normed = [sem(f"out_normed{l}") for l in range(2)]
        gate_ready = sem("gate_ready")
        up_ready = sem("up_ready")
        gelu_done = sem("gelu_done")
        hidden_done = sem("hidden_done")
        down_ready = sem("down_ready")
        result_ready = sem("result_ready")
        out_stored = sem("out_stored")

        QKV_DMAS = [3, 5]
        SPLITS = PERIOD + 8

        def split_number(A, unit_u, name):
            return sum(1 for (u, n), k in A.number.items() if n[0] in "qk" and k < A.number[unit_u, name])

        def job_bank(A, unit, name):
            return four_banks[A.number[-1, name] % 4] if unit.u < 0 and name[0] != "r" else work_bank

        block = ctx.enter_context(nc.Block())

        @block.sync
        def _(sp):
            def load_qkv(l, b, cols):
                s = qkv_loaded[l][b]
                sp.dma_start(w_q[l][b][:, :, :], wq_dram[l][:, :, cols]).then_inc(s, 16)
                for w, dram in ((w_k, (Wk1, Wk2)[l]), (w_v, (Wv1, Wv2)[l])):
                    if l == 0:
                        sp.dma_start(w[l][b][:, :, :],
                                     dram.rearrange("(c p) n -> p c n", p=P)[:, :, cols]).then_inc(s, 16)
                    else:
                        for c, rows in enumerate(cross_attn.key_rows):
                            sp.dma_start(w[l][b][0:rows, c, :], dram[c * P:c * P + rows, cols]).then_inc(s, 16)

            for g in range(4):
                sp.dma_start(x_sb[:, 4 * g:4 * g + 4, :], x_dram[:, 4 * g:4 * g + 4, :]).then_inc(x_loaded[g], 16)
            for n, (g, b) in enumerate(((g1, b1), (g2, b2), (g3, b3))):
                sp.dma_start(gains[:, n, :], g.rearrange("(c p) -> p c", p=P), allow_slow_non_contiguous=True).then_inc(vec_loaded, 16)
                sp.dma_start(shifts[:, n, :], b.rearrange("(c p) -> p c", p=P), allow_slow_non_contiguous=True).then_inc(vec_loaded, 16)
            for n, b in enumerate((bo1, bo2, bf)):
                sp.dma_start(bias_b[:, n, :], b.partition_broadcast(P)).then_inc(vec_loaded, 16)
            sp.dma_start(bp_sb[:, :], bp.rearrange("(f p) -> p f", p=P), allow_slow_non_contiguous=True).then_inc(vec_loaded, 16)
            load_qkv(0, 0, slice(0, P))
            full = (CTX_TILES - 1) * P
            sp.dma_start(ctx_stage[:, 0:CTX_TILES - 1, :],
                         ctx_rows[0:full, :].rearrange("(t p) d -> p t d", p=P)).then_inc(ctx_loaded, 16)
            sp.dma_start(ctx_stage[0:CTX_LAST, CTX_TILES - 1, :], ctx_rows[full:CTX_TOKENS, :]).then_inc(ctx_loaded, 16)
            load_qkv(0, 1, slice(P, 2 * P))
            for l in range(2):
                for b in range(2):
                    sp.dma_start(w_o[l][b][:, :], wo_dram[l][:, b, :]).then_inc(wo_loaded[l][b], 16)
            for b in range(2):
                load_qkv(1, b, slice(b * P, b * P + P))
            def attention(l, A):
                def job(unit, name):
                    nxt = unit.u + 1
                    if name == "q":
                        sp.wait_ge(hi_ready[l], unit.at(split_number(A, unit.u, name) + 1, SPLITS))
                        for a in range(2):
                            q = q_hi[nxt % 2][a]
                            sp.dma_start(q[HALF:P, :].bitcast(FP32), q[0:HALF, :].bitcast(FP32)).then_inc(queries_doubled[l], 16)
                    elif name[0] == "k":
                        sp.wait_ge(hi_ready[l], unit.at(split_number(A, unit.u, name) + 1, SPLITS))
                        start, width = A.key_chunks[int(name[1])]
                        b = (unit.u // CHUNKS + 1) % 2
                        for a in range(2):
                            sp.dma_start(k_hi_one[b][a][0:HALF, start:start + width].bitcast(FP32),
                                         k_hi_lo[b][a][0:HALF, start:start + width].bitcast(FP32)).then_inc(keys_doubled[l], 16)
                    elif name[:3] == "row":
                        a = int(name[3])
                        sp.wait_ge(work_taken[l], A.job(unit, name) + 1)
                        for i in range(Q_TILES):
                            sp.dma_start(q_lo[nxt % 2][a][HALF:HALF + 1, i * P:(i + 1) * P].bitcast(FP32),
                                         max_rows[a][i:i + 1, :].bitcast(FP32)).then_inc(rows_placed[l][a], 16)

                before = Unit(-1)
                for name in ("k0", "k1", "k2", "k3", "q", "row0", "row1"):
                    job(before, name)
                for unit in units(sp):
                    for t in range(A.steps):
                        for name in A.jobs_at(unit, t):
                            job(unit, name)
                            if name == "q" and unit.chunk == 2 and unit.u // CHUNKS + 2 < PAIRS:
                                sp.wait_ge(work_ready[l], A.job(unit, "q") + 1)
                                b = unit.pair_parity
                                load_qkv(l, b, bass.ds(unit.at((unit.u // CHUNKS + 2) * P, 2 * P), P))
                            if name == "y1" and unit.chunk == 0 and unit.u >= CHUNKS and unit.has_next_pair:
                                sp.wait_ge(work_ready[l], A.job(unit, "y1") + 1)
                                pair = unit.u // CHUNKS + 1
                                sp.dma_start(w_o[l][pair % 2][:, :], wo_dram[l][:, bass.ds(unit.at(pair, 2), 1), :]
                                             .rearrange("p r n -> p (r n)")).then_inc(wo_loaded[l][pair % 2], 16)

            for l, A in enumerate(layers):
                attention(l, A)
            sp.wait_ge(scores_ready[1], 2 * UNITS * cross_attn.steps)
            sp.dma_start(w_p[:, :, :], Wp.rearrange("(c p) n -> p c n", p=P)).then_inc(ff_loaded, 16)
            sp.dma_start(w_f[:, :, :], Wf.rearrange("(f p) n -> p f n", p=P)).then_inc(ff_loaded, 16)
            with sp.Fori(0, CHUNKS) as q:
                sp.wait_ge(result_ready, q * 2 + 2)
                sp.dma_start(out_dram[:, bass.ds(q * 4, 4), :], x_sb[:, bass.ds(q * 4, 4), :]).then_inc(out_stored, 16)
            sp.wait_ge(out_stored, 16 * CHUNKS)

        @block.gpsimd
        def _(pool):
            nc.gpsimd.memset(ident[:, :], 0.0).then_inc(ident_zeroed, 1)
            pool.wait_ge(ident_zeroed, 1)
            nc.gpsimd.affine_select(out=ident[:, :], in_=ident[:, :], compare_op=ALU.not_equal, fill=1.0,
                                    base=0, pattern=[[-1, P]], channel_multiplier=1).then_inc(ident_ready, 1)

            def add_bias(n):
                pool.wait_ge(vec_loaded, 160)
                for g in range(4):
                    pool.wait_ge(normalised, TOKEN_TILES * n + 4 * g + 4)
                    nc.gpsimd.tensor_tensor(
                        x_sb[:, 4 * g:4 * g + 4, :], x_sb[:, 4 * g:4 * g + 4, :],
                        bias_b[:, n:n + 1, :].to_broadcast([P, 4, DIM]), ALU.add).then_inc(bias_added, 1)

            def attention(l, A):
                for unit in units(pool):
                    for n, group in enumerate(A.pool_adds):
                        s = group[-1]
                        rows = A.tile_keys[s]
                        slots = [(unit.u * A.steps + t) % RING for t in group]
                        if n == 0 and not unit.first:
                            pool.wait_ge(sums_merged[l], unit.at(unit.u, PERIOD))
                        if n > 0:
                            pool.wait_ge(pool_added[l], unit.at(unit.u * len(A.pool_adds) + n,
                                                                PERIOD * len(A.pool_adds)))
                        pool.wait_ge(probs_ready[l], unit.at(2 * (unit.u * A.steps + s) + 2, 2 * PERIOD * A.steps))
                        first = probs[0:rows, slots[0], :, :] if n == 0 else pool_sum[0:rows, :, :]
                        nc.gpsimd.tensor_tensor(pool_sum[0:rows, :, :], first, probs[0:rows, slots[-1], :, :],
                                                ALU.add).then_inc(pool_added[l], 1)

            add_bias(0)
            attention(0, self_attn)
            add_bias(1)
            attention(1, cross_attn)
            add_bias(2)

        @block.tensor
        def _(pe):
            def layer_norm(n):
                if n == 0:
                    pe.wait_ge(ident_ready, 1)
                for g in range(4):
                    for c in range(DIM_TILES):
                        k = 2 * g + c
                        wait(pe, xn_ready, 8 * n + k - 3 if k > 3 else 0)
                        for j in range(4):
                            pe.wait_ge(normalised, TOKEN_TILES * n + 4 * g + j + 1)
                            last = nc.tensor.transpose(four_banks[k % 4][:, j * P:(j + 1) * P],
                                                       xn_stage[:, 4 * g + j, c * P:(c + 1) * P], ident[:, :])
                        last.then_inc(xn_turned, 1)

            def turn_context():
                pe.wait_ge(ctx_loaded, 32)
                for g in range(4):
                    for c, rows in enumerate(cross_attn.key_rows):
                        k = 2 * g + c
                        pe.wait_ge(xn_ready, 8)
                        wait(pe, ctx_ready, k - 3)
                        for t in range(4 * g, min(4 * g + 4, CTX_TILES)):
                            m = cross_attn.tile_keys[t]
                            last = nc.tensor.transpose(
                                four_banks[k % 4][0:rows, (t - 4 * g) * P:(t - 4 * g) * P + m],
                                ctx_stage[0:m, t, c * P:c * P + rows], ident[0:m, 0:m])
                        last.then_inc(ctx_turned, 1)

            def attention(l, A):
                src = xn_t if l == 0 else ctx_t

                def scores(unit, t):
                    m = A.tile_keys[t]
                    cols = slice(t * P, t * P + m)
                    for a in range(2):
                        k_both, k_one = k_hi_lo[unit.pair_parity][a], k_hi_one[unit.pair_parity][a]
                        dst = score_banks[a][0:m, :]
                        if not (unit.first and t == 0):
                            pe.wait_ge(probs_ready[l], unit.at(2 * (unit.u * A.steps + t - 1) + a + 1,
                                                               2 * PERIOD * A.steps))
                        nc.tensor.matmul(dst, k_both[:, cols], q_hi[unit.parity][a][:, :], start=True, stop=False)
                        if t == 0:
                            pe.wait_ge(rows_placed[l][a], unit.at(64 * (unit.u + 1), 64 * PERIOD))
                            if unit.chunk == 0 and a == 0:
                                pe.wait_ge(keys_doubled[l], unit.at(128 * (unit.u // CHUNKS + 1), 256))
                        nc.tensor.matmul(dst, k_one[:, cols], q_lo[unit.parity][a][:, :],
                                         start=False, stop=True).then_inc(scores_ready[l], 1)
                        yield

                def weighted_values(unit, t):
                    m = A.tile_keys[t]
                    slot = (unit.u * A.steps + t) % RING
                    pe.wait_ge(probs_ready[l], unit.at(2 * (unit.u * A.steps + t) + 2, 2 * PERIOD * A.steps))
                    if t == 0 and not unit.first:
                        pe.wait_ge(out_copied[l], unit.at(unit.u, PERIOD))
                        if unit.chunk == 0:
                            pe.wait_ge(work_taken[l], unit.at(A.number[unit.u - 1, "v3"] + 1, A.period_jobs))
                    for a in range(2):
                        last = nc.tensor.matmul(out_bank[a * HALF:(a + 1) * HALF, :],
                                                v_sb[0:m, unit.pair_parity, t, a * HALF:(a + 1) * HALF],
                                                probs[0:m, slot, a, :], start=(t == 0), stop=(t == A.steps - 1))
                    last.then_inc(values_used[l], 1)

                def max_tile(unit, n):
                    nxt = unit.u + 1
                    a, i, kc = n // 16, n // 4 % 4, n % 4
                    start, width = A.max_chunks[kc]
                    dst = max_banks[n % 4][:, 0:width]
                    if not (unit.u == -1 and n < 4):
                        pe.wait_ge(max_tile_taken[l], unit.at(MAX_TILES * nxt + n - 3, PERIOD * MAX_TILES))
                    if n == 0:
                        pe.wait_ge(work_taken[l], A.job(unit, "q") + 1)
                        pe.wait_ge(queries_doubled[l], unit.at(32 * (nxt + 1), 32 * PERIOD))
                    nc.tensor.matmul(dst, q_hi[nxt % 2][a][:, i * P:(i + 1) * P],
                                     k_hi_lo[(nxt // CHUNKS) % 2][a][:, start:start + width],
                                     start=True, stop=True).then_inc(max_tile_ready[l], 1)

                def job(unit, name):
                    n = A.job(unit, name)
                    work = job_bank(A, unit, name)
                    if unit.u < 0 and name[0] != "r":
                        wait(pe, work_taken[l], n - 3 if name[0] in "kq" else max(n - 3, A.number[-1, "v0"]))
                    else:
                        wait(pe, work_taken[l], n)
                    nxt = unit.u + 1
                    pair = (unit.u // CHUNKS + 1)
                    if name == "q":
                        chunk = nxt % CHUNKS
                        for c in range(DIM_TILES):
                            last = nc.tensor.matmul(work[:, :], w_q[l][(nxt // CHUNKS) % 2][:, c, :],
                                                    xn_t[:, c, chunk * BANK:(chunk + 1) * BANK],
                                                    start=(c == 0), stop=(c == DIM_TILES - 1))
                    elif name[0] == "k":
                        if name == "k0":
                            pe.wait_ge(qkv_loaded[l][pair % 2],
                                       unit.at(16 * QKV_DMAS[l] * (pair // 2 + 1), 16 * QKV_DMAS[l]))
                        start, width = A.key_chunks[int(name[1])]
                        for c, rows in enumerate(A.key_rows):
                            last = nc.tensor.matmul(work[:, 0:width], w_k[l][pair % 2][0:rows, c, :],
                                                    src[0:rows, c, start:start + width],
                                                    start=(c == 0), stop=(c == DIM_TILES - 1))
                    elif name[0] == "v":
                        for t in range(4 * int(name[1]), min(4 * int(name[1]) + 4, A.steps)):
                            m = A.tile_keys[t]
                            for c, rows in enumerate(A.key_rows):
                                last = nc.tensor.matmul(work[0:m, (t % 4) * P:(t % 4 + 1) * P],
                                                        src[0:rows, c, t * P:t * P + m],
                                                        w_v[l][pair % 2][0:rows, c, :],
                                                        start=(c == 0), stop=(c == DIM_TILES - 1))
                    elif name == "sum":
                        pe.wait_ge(sums_merged[l], unit.at(unit.u, PERIOD))
                        prev = (unit.u - 1) % 2
                        for a in range(2):
                            last = nc.tensor.matmul(work[a * HALF:(a + 1) * HALF, :], ones[:, 0:HALF],
                                                    dve_sum[:, prev, a, :], start=True, stop=True)
                    elif name[0] == "y":
                        prev_pair = (unit.u - 1) // CHUNKS
                        if name == "y0":
                            pe.wait_ge(out_normed[l], unit.at(unit.u, PERIOD))
                            if (unit.u - 1) % CHUNKS == 0:
                                pe.wait_ge(wo_loaded[l][prev_pair % 2], unit.at(16 * (prev_pair // 2 + 1), 16))
                        for k in range(2):
                            i = 2 * int(name[1]) + k
                            last = nc.tensor.matmul(work[:, k * DIM:(k + 1) * DIM], o_norm[:, i * P:(i + 1) * P],
                                                    w_o[l][prev_pair % 2][:, :], start=True, stop=True)
                    else:
                        a = int(name[3])
                        pe.wait_ge(head_max_ready[l], unit.at(2 * nxt + a + 1, 2 * PERIOD))
                        last = nc.tensor.transpose(work[0:Q_TILES, 0:P],
                                                   query_max[:, a * Q_TILES:(a + 1) * Q_TILES], ident[:, :])
                    last.then_inc(work_ready[l], 1)

                before = Unit(-1)
                pe.wait_ge(xn_ready, 8 * (l + 1))
                if l == 0:
                    pe.wait_ge(ctx_ready, 8)
                    pe.wait_ge(key_ones, 4)
                pe.wait_ge(consts_set, 1)
                for name in ("k0", "k1", "k2", "k3", "q", "v0", "v1", "v2", "v3"):
                    job(before, name)
                for n in range(MAX_TILES):
                    max_tile(before, n)
                job(before, "row0")
                job(before, "row1")
                for unit in units(pe):
                    for t in range(A.steps):
                        tiles = list(A.max_at[t]) if unit.has_next else []
                        for _ in scores(unit, t):
                            if tiles and tiles[0] > 0:
                                max_tile(unit, tiles.pop(0))
                        for name in A.jobs_at(unit, t):
                            job(unit, name)
                        if t > 0:
                            weighted_values(unit, t - 1)
                        elif not unit.first:
                            weighted_values(Unit(unit.u - 1, unit.i), A.steps - 1)
                        for n in tiles:
                            max_tile(unit, n)
                weighted_values(unit, A.steps - 1)
                after = Unit(UNITS)
                for name in ("sum", "y0", "y1"):
                    job(after, name)

            layer_norm(0)
            turn_context()
            attention(0, self_attn)
            layer_norm(1)
            attention(1, cross_attn)
            layer_norm(2)

            pe.wait_ge(xn_ready, 24)
            pe.wait_ge(ff_loaded, 32)

            def feed_forward(q):
                for f in range(FF_TILES):
                    gate, up = four_banks[2 * (f % 2)], four_banks[2 * (f % 2) + 1]
                    wait(pe, hidden_done, q * FF_TILES + (f - 1))
                    for dst, col, s in ((gate, FF + f * P, gate_ready), (up, f * P, up_ready)):
                        for c in range(DIM_TILES):
                            last = nc.tensor.matmul(dst[:, :], w_p[:, c, col:col + P],
                                                    xn_t[:, c, bass.ds(q * BANK, BANK)],
                                                    start=(c == 0), stop=(c == DIM_TILES - 1))
                        last.then_inc(s, 1)
                for j in range(2):
                    wait(pe, result_ready, q * 2 + (j - 1))
                    pe.wait_ge(hidden_done, q * FF_TILES + FF_TILES)
                    for k in range(2):
                        i = 2 * j + k
                        for f in range(FF_TILES):
                            last = nc.tensor.matmul(max_banks[j][:, k * DIM:(k + 1) * DIM],
                                                    hidden[:, f, i * P:(i + 1) * P], w_f[:, f, :],
                                                    start=(f == 0), stop=(f == FF_TILES - 1))
                    last.then_inc(down_ready, 1)

            feed_forward(0)
            with pe.Fori(1, CHUNKS) as q:
                feed_forward(q)

        @block.scalar
        def _(act):
            def layer_norm(n):
                act.wait_ge(consts_set, 1)
                for g in range(4):
                    act.wait_ge(moments_done, TOKEN_TILES * n + 4 * g + 4)
                    nc.scalar.activation(std[:, 4 * g:4 * g + 4], moments[:, 4 * g:4 * g + 4, 1], ACT.Sqrt,
                                         bias=eps_col[:, :]).then_inc(std_done, 1)
                if n == 0:
                    act.wait_ge(vec_loaded, 160)
                for g in range(4):
                    for c in range(DIM_TILES):
                        k = 2 * g + c
                        act.wait_ge(xn_turned, 8 * n + k + 1)
                        nc.scalar.activation(xn_t[:, c, g * BANK:(g + 1) * BANK], four_banks[k % 4][:, :],
                                             ACT.Identity, bias=shifts[:, n, c:c + 1],
                                             scale=gains[:, n, c:c + 1]).then_inc(xn_ready, 1)

            def take_context():
                for g in range(4):
                    for c, rows in enumerate(cross_attn.key_rows):
                        k = 2 * g + c
                        width = min(BANK, CTX_TOKENS - g * BANK)
                        act.wait_ge(ctx_turned, k + 1)
                        nc.scalar.copy(ctx_t[0:rows, c, g * BANK:g * BANK + width],
                                       four_banks[k % 4][0:rows, 0:width]).then_inc(ctx_ready, 1)

            def attention(l, A):
                def exp(unit, t):
                    m = A.tile_keys[t]
                    slot = (unit.u * A.steps + t) % RING
                    for a in range(2):
                        act.wait_ge(scores_ready[l], unit.at(2 * (unit.u * A.steps + t) + a + 1,
                                                             2 * PERIOD * A.steps))
                        if a == 0 and not (unit.first and t < RING):
                            act.wait_ge(values_used[l], unit.at(unit.u * A.steps + t - RING + 1, PERIOD * A.steps))
                            kind, adds = A.adder(unit, t - RING)
                            act.wait_ge({"dve": dve_added, "pool": pool_added}[kind][l], adds)
                        src = score_banks[a][0:m, :]
                        nc.scalar.activation(probs[0:m, slot, a, :], src, ACT.Exp,
                                             scale=SCALE).then_inc(probs_ready[l], 1)

                def job(unit, name):
                    if name[0] not in "qkvr":
                        return
                    act.wait_ge(work_ready[l], A.job(unit, name) + 1)
                    work = job_bank(A, unit, name)
                    nxt = unit.u + 1
                    pair_parity = (unit.u // CHUNKS + 1) % 2
                    if name == "q":
                        for a in range(2):
                            src = work[a * HALF:(a + 1) * HALF, :]
                            last = nc.scalar.copy(q_hi[nxt % 2][a][0:HALF, :], src)
                        last.then_inc(hi_ready[l], 1)
                    elif name[0] == "k":
                        start, width = A.key_chunks[int(name[1])]
                        for a in range(2):
                            src = work[a * HALF:(a + 1) * HALF, 0:width]
                            last = nc.scalar.copy(k_hi_lo[pair_parity][a][0:HALF, start:start + width], src)
                        last.then_inc(hi_ready[l], 1)
                    elif name[0] == "v":
                        t0 = 4 * int(name[1])
                        tiles = min(4, A.steps - t0)
                        m = A.tile_keys[t0]
                        nc.scalar.copy(v_sb[0:m, pair_parity, t0:t0 + tiles, :],
                                       work[0:m, 0:tiles * P].rearrange("p (t n) -> p t n", n=P)
                                       ).then_inc(work_taken[l], 1)
                    else:
                        nc.scalar.mul(max_rows[int(name[3])][:, :], work[0:Q_TILES, 0:P],
                                      -1.0).then_inc(work_taken[l], 1)

                def copy_out(unit):
                    act.wait_ge(values_used[l], unit.at(unit.u * A.steps, PERIOD * A.steps))
                    nc.scalar.copy(o_raw[:, (unit.u - 1) % 2, :], out_bank[:, :]).then_inc(out_copied[l], 1)

                before = Unit(-1)
                for name in ("k0", "k1", "k2", "k3", "q", "v0", "v1", "v2", "v3", "row0", "row1"):
                    job(before, name)
                for unit in units(act):
                    for t in range(A.steps):
                        exp(unit, t)
                        for name in A.jobs_at(unit, t):
                            job(unit, name)
                        if t == 0 and not unit.first:
                            copy_out(unit)
                copy_out(Unit(UNITS))

            layer_norm(0)
            take_context()
            act.wait_ge(consts_set, 1)
            for b in range(2):
                for a in range(2):
                    for n in range(TOKENS // BANK):
                        last = nc.scalar.copy(k_hi_one[b][a][HALF:HALF + 1, n * BANK:(n + 1) * BANK], one_row[:, :])
                    last.then_inc(key_ones, 1)
            attention(0, self_attn)
            layer_norm(1)
            attention(1, cross_attn)
            layer_norm(2)

            def gelu(q):
                for f in range(FF_TILES):
                    wait(act, gate_ready, q * FF_TILES + (f + 1))
                    wait(act, hidden_done, q * FF_TILES + (f - 1))
                    nc.scalar.activation(gelu_sb[:, f % 2, :], four_banks[2 * (f % 2)][:, :], ACT.Gelu,
                                         bias=bp_sb[:, FF_TILES + f:FF_TILES + f + 1]).then_inc(gelu_done, 1)

            gelu(0)
            with act.Fori(1, CHUNKS) as q:
                gelu(q)

        @block.vector
        def _(dve):
            nc.vector.memset(ones[:, :], 1.0)
            nc.vector.memset(one_row[:, :], 1.0)
            nc.vector.memset(eps_col[:, :], EPS).then_inc(consts_set, 1)

            def layer_norm(n):
                if n > 0:
                    dve.wait_ge(work_taken[n - 1], layers[n - 1].all_jobs)
                for g in range(4):
                    if n == 0:
                        dve.wait_ge(x_loaded[g], 16)
                    for t in range(4 * g, 4 * g + 4):
                        nc.vector.bn_stats(stats[:, t, :], x_sb[:, t, :]).then_inc(stats_done, 1)
                    for t in range(4 * g, 4 * g + 4):
                        dve.wait_ge(stats_done, TOKEN_TILES * n + t + 1)
                        nc.vector.bn_aggr(moments[:, t, :], stats[:, t, :]).then_inc(moments_done, 1)
                for g in range(4):
                    dve.wait_ge(std_done, 4 * n + g + 1)
                    nc.vector.reciprocal(rstd[:, 4 * g:4 * g + 4], std[:, 4 * g:4 * g + 4]).then_inc(rstd_done, 1)
                    dve.wait_ge(rstd_done, 4 * n + g + 1)
                    for t in range(4 * g, 4 * g + 4):
                        nc.vector.tensor_scalar(xn_stage[:, t, :], x_sb[:, t, :], moments[:, t, 0:1],
                                                rstd[:, t:t + 1], ALU.subtract, ALU.mult).then_inc(normalised, 1)

            def attention(l, A):
                def take_max(unit, n):
                    nxt = unit.u + 1
                    a, j, kc = n // 16, n // 4, n % 4
                    width = A.max_chunks[kc][1]
                    dve.wait_ge(max_tile_ready[l], unit.at(MAX_TILES * nxt + n + 1, PERIOD * MAX_TILES))
                    nc.vector.tensor_reduce(part_max[:, j, kc:kc + 1], max_banks[n % 4][:, 0:width], AX.X,
                                            ALU.max).then_inc(max_tile_taken[l], 1)
                    if n % 16 == 15:
                        dve.wait_ge(max_tile_taken[l], unit.at(MAX_TILES * nxt + n + 1, PERIOD * MAX_TILES))
                        heads = slice(a * Q_TILES, (a + 1) * Q_TILES)
                        nc.vector.tensor_reduce(query_max[:, heads], part_max[:, heads, :], AX.X,
                                                ALU.max).then_inc(head_max_ready[l], 1)

                def add_probs(unit, n):
                    group = A.dve_adds[n]
                    s = group[-1]
                    rows = A.tile_keys[s]
                    slots = [(unit.u * A.steps + t) % RING for t in group]
                    sums = dve_sum[0:rows, unit.parity, :, :]
                    dve.wait_ge(probs_ready[l], unit.at(2 * (unit.u * A.steps + s) + 2, 2 * PERIOD * A.steps))
                    if n > 0:
                        dve.wait_ge(dve_added[l], unit.at(unit.u * len(A.dve_adds) + n, PERIOD * len(A.dve_adds)))
                    first = probs[0:rows, slots[0], :, :] if n == 0 else sums
                    nc.vector.tensor_tensor(sums, first, probs[0:rows, slots[-1], :, :],
                                            ALU.add).then_inc(dve_added[l], 1)

                def merge_sums(unit):
                    sums = dve_sum[:, (unit.u - 1) % 2, :, :]
                    dve.wait_ge(pool_added[l], unit.at(unit.u * len(A.pool_adds), PERIOD * len(A.pool_adds)))
                    dve.wait_ge(dve_added[l], unit.at(unit.u * len(A.dve_adds), PERIOD * len(A.dve_adds)))
                    nc.vector.tensor_tensor(sums, sums, pool_sum[:, :, :], ALU.add).then_inc(sums_merged[l], 1)

                def job(unit, name):
                    nxt = unit.u + 1
                    work = job_bank(A, unit, name)
                    if name[0] in "qk":
                        pair_parity = (unit.u // CHUNKS + 1) % 2
                        dve.wait_ge(hi_ready[l], unit.at(split_number(A, unit.u, name) + 1, SPLITS))
                        for a in range(2):
                            if name == "q":
                                hi = q_hi[nxt % 2][a][0:HALF, :]
                                lo, width = q_lo[nxt % 2][a][0:HALF, :], BANK
                            else:
                                start, width = A.key_chunks[int(name[1])]
                                both = k_hi_lo[pair_parity][a]
                                hi, lo = both[0:HALF, start:start + width], both[HALF:P, start:start + width]
                            last = nc.vector.tensor_tensor(lo, work[a * HALF:(a + 1) * HALF, 0:width],
                                                           hi.bitcast(FP32), ALU.subtract)
                        last.then_inc(work_taken[l], 1)
                    elif name == "sum":
                        dve.wait_ge(work_ready[l], A.job(unit, name) + 1)
                        for part in range(4):
                            cols = slice(part * P, (part + 1) * P)
                            last = nc.vector.reciprocal(sum_recip[:, cols], work[:, cols])
                            if part < 3:
                                yield
                        last.then_inc(work_taken[l], 1)
                        dve.wait_ge(work_taken[l], A.job(unit, name) + 1)
                        dve.wait_ge(out_copied[l], unit.at(unit.u, PERIOD))
                        nc.vector.tensor_tensor(o_norm[:, :], o_raw[:, (unit.u - 1) % 2, :], sum_recip[:, :],
                                                ALU.mult).then_inc(out_normed[l], 1)
                    elif name[0] == "y":
                        t = 4 * ((unit.u - 1) % CHUNKS) + 2 * int(name[1])
                        rows = x_sb[:, t:t + 2, :]
                        dve.wait_ge(work_ready[l], A.job(unit, name) + 1)
                        nc.vector.tensor_tensor(rows, rows, work[:, :].rearrange("p (t d) -> p t d", d=DIM),
                                                ALU.add).then_inc(work_taken[l], 1)

                def finish(parts):
                    for _ in parts:
                        pass

                before = Unit(-1)
                for name in ("k0", "k1", "k2", "k3", "q"):
                    finish(job(before, name))
                for n in range(MAX_TILES):
                    take_max(before, n)
                late_job = None
                for unit in units(dve):
                    if unit.u == 0:
                        dve.wait_ge(bias_added, 4 * l + 4)
                    for t in range(A.steps):
                        tiles = list(A.max_at[t]) if unit.has_next else []
                        if t == 2 and not unit.first:
                            merge_sums(unit)
                        for n in tiles:
                            take_max(unit, n)
                        if late_job and not any(name[0] == "k" for name in A.jobs_at(unit, t)):
                            finish(late_job)
                            late_job = None
                        for name in A.jobs_at(unit, t):
                            if name[0] == "k" and t < A.steps - 1:
                                late_job = job(unit, name)
                                continue
                            pending = job(unit, name)
                            next(pending, None)
                            if name == "sum":
                                recips = pending
                        if 4 < t < 8 and not unit.first:
                            next(recips, None)
                        for n, group in enumerate(A.dve_adds):
                            if group[-1] == t - 1:
                                add_probs(unit, n)
                after = Unit(UNITS)
                merge_sums(after)
                for name in ("sum", "y0", "y1"):
                    finish(job(after, name))

            layer_norm(0)
            attention(0, self_attn)
            layer_norm(1)
            attention(1, cross_attn)
            layer_norm(2)

            def feed_forward(q):
                for f in range(FF_TILES):
                    dve.wait_ge(up_ready, q * FF_TILES + (f + 1))
                    dve.wait_ge(gelu_done, q * FF_TILES + (f + 1))
                    wait(dve, down_ready, q * 2)
                    nc.vector.scalar_tensor_tensor(hidden[:, f, :], four_banks[2 * (f % 2) + 1][:, :],
                                                   bp_sb[:, f:f + 1], gelu_sb[:, f % 2, :], ALU.add,
                                                   ALU.mult).then_inc(hidden_done, 1)
                for j in range(2):
                    dve.wait_ge(down_ready, q * 2 + (j + 1))
                    rows = x_sb[:, bass.ds(q * 4 + 2 * j, 2), :]
                    nc.vector.tensor_tensor(rows, rows, max_banks[j][:, :].rearrange("p (t d) -> p t d", d=DIM),
                                            ALU.add).then_inc(result_ready, 1)

            dve.wait_ge(bias_added, 12)
            feed_forward(0)
            with dve.Fori(1, CHUNKS) as q:
                feed_forward(q)


_PREFIX = "L0_xattn_"
_NAMES = ["Wq1", "Wk1", "Wv1", "Wo1", "bo1", "Wq2", "Wk2", "Wv2", "Wo2", "bo2", "Wp", "bp", "Wf", "bf",
          "g1", "b1", "g2", "b2", "g3", "b3"]
_INS = ["x", "ctx_768"] + [_PREFIX + n for n in _NAMES]


def kernel(**inputs):
    import numpy as _np
    import concourse.bacc as _bacc
    from concourse import mybir as _mybir
    from concourse.bass_utils import run_bass_kernel_spmd as _run

    nc = _bacc.Bacc("TRN2", target_bir_lowering=False, num_devices=1)
    arrays, args = {}, []
    for name in _INS:
        a = _np.ascontiguousarray(inputs[name])
        arrays[f"in_{name}_dram"] = a
        args.append(nc.dram_tensor(f"in_{name}_dram", a.shape, _mybir.dt.from_np(a.dtype), kind="ExternalInput").ap())
    out = nc.dram_tensor("out_dram", (1, TOKENS, DIM), _mybir.dt.float32, kind="ExternalOutput").ap()
    xattn_block(nc, *args, out)
    r = _run(nc, [arrays], core_ids=[0])
    return r.results[0]["out_dram"]
```

```python
from contextlib import ExitStack

import concourse.bass as bass
from concourse import mybir

FP32 = mybir.dt.float32
FP32R = mybir.dt.float32r
ALU = mybir.AluOpType
ACT = mybir.ActivationFunctionType
AX = mybir.AxisListType

P = 128
HALF = P // 2
BANK = 512
TOKENS, DIM, CTX_TOKENS, CTX_DIM = 2048, 256, 1601, 192
HEADS, HEAD_DIM = 16, 64
INNER = HEADS * HEAD_DIM
FF = 1024
EPS = 1e-5
SCALE = HEAD_DIM ** -0.5
DIM_TILES = DIM // P
TOKEN_TILES = TOKENS // P
CHUNKS = TOKENS // BANK
PAIRS = HEADS // 2
UNITS = PAIRS * CHUNKS
PERIOD = 2 * CHUNKS
Q_TILES = BANK // P
MAX_TILES = 2 * Q_TILES * 4
RING = 4
CTX_TILES = -(-CTX_TOKENS // P)
CTX_LAST = CTX_TOKENS - (CTX_TILES - 1) * P
FF_TILES = FF // P


class Unit:

    def __init__(self, layer, u, i=None):
        self.layer, self.u, self.i = layer, u, i
        self.overall = layer * UNITS + u
        self.chunk = u % CHUNKS
        self.parity = u % 2
        self.pair_parity = (u // CHUNKS) % 2
        self.first = layer == 0 and u == 0
        ahead = i is not None or layer == 0
        self.has_next = ahead or u < UNITS - 1
        self.has_next_pair = ahead or u < UNITS - CHUNKS
        self.next_layer = min(layer + (u == UNITS - 1), 1)
        self.next_pair_layer = min(layer + (u >= UNITS - CHUNKS), 1)
        self.next = (u + 1) % UNITS
        self.next_pair = (u // CHUNKS + 1) % PAIRS
        self.prev_layer = layer - (u == 0)
        self.prev_pair = ((u - 1) // CHUNKS) % PAIRS

    def at(self, value, per_period):
        return value if self.i is None else self.i * per_period + value

    def norm(self, half):
        if self.i is None:
            return {(0, 30, 0): (1, 0), (0, 31, 0): (1, 1), (1, 0, 0): (1, 2), (1, 0, 1): (1, 3),
                    (1, 30, 0): (2, 0), (1, 31, 0): (2, 1), (1, 31, 1): (2, 2), (1, 32, 0): (2, 3),
                    }.get((self.layer, self.u, half))


def units(eng, layer):
    yield Unit(layer, 0)
    loops = (UNITS - 1) // PERIOD
    with eng.Fori(0, loops) as i:
        for u in range(1, PERIOD + 1):
            yield Unit(layer, u, i)
    for u in range(1 + loops * PERIOD, UNITS):
        yield Unit(layer, u)


class Attention:

    def __init__(self, layer, keys, key_chunks, max_chunks, key_rows, slots, recip_steps, max_steps, dve_adds,
                 norm_slots=None, norm_recip_steps=None):
        self.layer, self.keys = layer, keys
        self.steps = -(-keys // P)
        self.tile_keys = [min(P, keys - t * P) for t in range(self.steps)]
        self.key_chunks = key_chunks
        self.max_chunks = max_chunks
        self.key_rows = key_rows
        self.slots = slots
        self.recip_steps = recip_steps
        self.norm_slots, self.norm_recip_steps = norm_slots or slots, norm_recip_steps or recip_steps
        assert sum(max_steps) == MAX_TILES and len(max_steps) == self.steps
        self.max_at = [list(range(sum(max_steps[:t]), sum(max_steps[:t + 1]))) for t in range(self.steps)]
        self.dve_adds = dve_adds
        self.adds = self.steps - 1

    def jobs_at(self, unit, t):
        names = []
        for slot, name in self.norm_slots if unit.norm(1) else self.slots:
            if slot == t:
                if name in ("q", "row0", "row1") and not unit.has_next:
                    continue
                if name in ("kv0", "kv1"):
                    if not unit.has_next_pair:
                        continue
                    which = 2 * (unit.chunk % 2) + int(name[2])
                    name = ("k" if unit.chunk < 2 else "v") + str(which)
                if name in ("sum", "y0", "y1") and unit.first:
                    continue
                if name[:2] == "ln" and not unit.norm(int(name[2]) // 2):
                    continue
                names.append(name)
        return names

    def recips_at(self, unit, t):
        steps = self.norm_recip_steps if unit.norm(1) else self.recip_steps
        return 0 if unit.first else steps.count(t)

    def added(self, unit, t):
        return unit.at(unit.u * self.adds + max(t, 1), PERIOD * self.adds)


FIRST_JOBS = ["k0", "k1", "k2", "k3", "q", "v0", "v1", "v2", "v3", "row0", "row1"]
LAST_JOBS = ["sum", "y0", "y1", "ln0", "ln1"]


class Jobs:

    def __init__(self, layers):
        order = [(0, -1, name) for name in FIRST_JOBS]
        for A in layers:
            for u in range(UNITS):
                for t in range(A.steps):
                    order += [(A.layer, u, name) for name in A.jobs_at(Unit(A.layer, u), t)]
        order += [(1, UNITS, name) for name in LAST_JOBS]
        self.numbers = {job: n for n, job in enumerate(order)}
        self.per_period = [self.numbers[l, PERIOD + 1, "q"] - self.numbers[l, 1, "q"] for l in range(2)]
        self.splits = {job: sum(1 for j in order[:n] if j[2][0] in "qk") for n, job in enumerate(order)}

    def number(self, unit, name):
        return unit.at(self.numbers[unit.layer, unit.u, name], self.per_period[unit.layer])

    def taken(self, unit, name, back=0):
        n = self.numbers[unit.layer, unit.u, name] - back
        return n % 2, unit.at(n // 2 + 1, self.per_period[unit.layer] // 2)

    def split(self, unit, name):
        return unit.at(self.splits[unit.layer, unit.u, name], PERIOD + 8)

    def last_turned(self, unit, half):
        turns = [n + 1 for job, n in self.numbers.items() if job[2] in ("ln1", "ln3")]
        number = self.numbers[unit.layer, unit.u, f"ln{2 * half}"]
        return max(n for n in turns if n <= number)

    def sums_read(self, unit):
        per_period = self.per_period[unit.layer]
        if unit.i is None:
            layer, u = (unit.layer, unit.u - 1) if unit.u > 0 else (0, UNITS - 1)
            return self.numbers[layer, u, "sum"] + 1
        if unit.u > 1:
            return unit.at(self.numbers[unit.layer, unit.u - 1, "sum"] + 1, per_period)
        return unit.at(self.numbers[unit.layer, PERIOD, "sum"] + 1 - per_period, per_period)


def wait(eng, sem, value):
    if not isinstance(value, int) or value > 0:
        eng.wait_ge(sem, value)


def xattn_block(nc, x, ctx_768, Wq1, Wk1, Wv1, Wo1, bo1, Wq2, Wk2, Wv2, Wo2, bo2, Wp, bp, Wf, bf,
                g1, b1, g2, b2, g3, b3, out):
    self_attn = Attention(
        0, TOKENS, [(BANK * j, BANK) for j in range(4)], [(BANK * j, BANK) for j in range(4)], [P, P],
        [(0, "q"), (1, "kv0"), (5, "kv1"), (7, "ln0"), (7, "ln1"), (8, "row0"), (8, "sum"), (13, "row1"),
         (14, "y0"), (15, "y1")],
        [9, 10, 12, 13],
        [0, 0, 2, 3, 3, 3, 3, 3, 3, 3, 3, 3, 3, 0, 0, 0], [])
    width = -(-CTX_TOKENS // 8) * 2
    cross_attn = Attention(
        1, CTX_TOKENS, [(BANK * j, min(BANK, CTX_TOKENS - BANK * j)) for j in range(4)],
        [(min(j * (width - 2), CTX_TOKENS - width), width) for j in range(4)], [P, CTX_DIM - P],
        [(0, "q"), (1, "kv0"), (2, "kv1"), (7, "ln0"), (7, "ln1"), (8, "row0"), (8, "sum"), (11, "row1"),
         (12, "y0"), (12, "y1")],
        [9, 10, 10, 11],
        [0, 0, 3, 4, 4, 4, 4, 4, 4, 4, 1, 0, 0], [],
        [(0, "q"), (2, "kv0"), (3, "sum"), (7, "ln0"), (7, "ln1"), (8, "y0"), (9, "y1"), (10, "row0"),
         (11, "row1"), (12, "kv1"), (12, "ln2"), (12, "ln3")],
        [4, 5, 5, 6])
    assert cross_attn.max_chunks[-1][0] + width == CTX_TOKENS
    layers = [self_attn, cross_attn]
    jobs = Jobs(layers)

    x_dram = x.rearrange("b (t p) d -> p (b t) d", p=P)
    out_dram = out.rearrange("b (t p) d -> p (b t) d", p=P)
    ctx_rows = ctx_768.rearrange("b t d -> (b t) d")
    wq_dram = [w.rearrange("(c p) n -> p c n", p=P) for w in (Wq1, Wq2)]
    wo_dram = [w.rearrange("(r p) n -> p r n", p=P) for w in (Wo1, Wo2)]

    ctx = ExitStack()
    with ctx:
        def sb(name, shape, dtype=FP32, stack=ctx):
            return stack.enter_context(nc.sbuf_tensor(name, shape, dtype))

        def sem(name):
            return ctx.enter_context(nc.semaphore(name))

        x_sb = sb("x_sb", [P, TOKEN_TILES, DIM])
        xn_t = sb("xn_t", [P, DIM_TILES, TOKENS])
        ctx_t = sb("ctx_t", [P, 2, CTX_TOKENS])
        q_hi = [[sb(f"q_hi{b}{a}", [P, BANK], FP32R) for a in range(2)] for b in range(2)]
        q_lo = [[sb(f"q_lo{b}{a}", [HALF + 1, BANK], FP32R) for a in range(2)] for b in range(2)]
        v_sb = sb("v_sb", [P, 2, TOKEN_TILES, P])
        probs = sb("probs", [P, RING, 2, BANK])
        sums = sb("sums", [P, 2, 2, BANK])
        w_q = [[sb(f"w_q{l}{b}", [P, DIM_TILES, P]) for b in range(2)] for l in range(2)]
        w_k = [[sb(f"w_k{l}{b}", [P, DIM_TILES, P]) for b in range(2)] for l in range(2)]
        w_v = [[sb(f"w_v{l}{b}", [P, DIM_TILES, P]) for b in range(2)] for l in range(2)]
        w_o = [[sb(f"w_o{l}{b}", [P, DIM]) for b in range(2)] for l in range(2)]
        o_raw = sb("o_raw", [P, 2, BANK])
        o_norm = sb("o_norm", [P, BANK])
        sum_recip = sb("sum_recip", [P, BANK])
        part_max = sb("part_max", [P, 2 * Q_TILES, 4])
        query_max = sb("query_max", [P, 2 * Q_TILES])
        max_rows = [sb(f"max_rows{a}", [Q_TILES, P], FP32R) for a in range(2)]
        ident = sb("ident", [P, P])
        ones = sb("ones", [P, P])
        one_row = sb("one_row", [1, BANK])
        eps_col = sb("eps_col", [P, 1])
        gains = sb("gains", [P, 3, DIM_TILES])
        shifts = sb("shifts", [P, 3, DIM_TILES])
        bias_b = sb("bias_b", [P, 3, DIM])
        bp_sb = sb("bp_sb", [P, 2 * FF_TILES])
        norm_stage = sb("norm_stage", [P, Q_TILES, DIM])
        stats = sb("stats", [P, TOKEN_TILES, 6])
        moments = sb("moments", [P, TOKEN_TILES, 2])
        std = sb("std", [P, TOKEN_TILES])
        rstd = sb("rstd", [P, TOKEN_TILES])
        attn_memory = ExitStack()
        k_hi_lo, k_hi_one = [], []
        for b in range(2):
            k_hi_lo.append([sb(f"k_hi_lo{b}{a}", [P, TOKENS], FP32R, attn_memory) for a in range(2)])
            k_hi_one.append([sb(f"k_hi_one{b}{a}", [HALF + 1, TOKENS], FP32R, attn_memory) for a in range(2)])
        attn_memory.close()
        w_p = sb("w_p", [P, DIM_TILES, 2 * FF])
        w_f = sb("w_f", [P, FF_TILES, DIM])
        gelu_sb = sb("gelu_sb", [P, 4, BANK])
        hidden = sb("hidden", [P, FF_TILES, BANK])

        xn_stage = probs[:, :, :, :].rearrange("p r a n -> p (r a n)").rearrange("p (t d) -> p t d", d=DIM)
        ctx_stage = v_sb[:, :, :, :].rearrange("p b t n -> p (b t n)")[:, 0:CTX_TILES * CTX_DIM].rearrange(
            "p (t d) -> p t d", d=CTX_DIM)

        def bank(name):
            return ctx.enter_context(nc.psum_tensor(name, [P, BANK], FP32))

        score_banks = [bank(f"scores{n}") for n in range(2)]
        max_banks = [bank(f"max_scores{n}") for n in range(3)]
        out_bank = bank("attn_out")
        work_banks = [bank(f"work{n}") for n in range(2)]
        four_banks = work_banks + score_banks
        ff_banks = max_banks + [out_bank]

        x_loaded = [sem(f"x_loaded{g}") for g in range(4)]
        ctx_loaded = sem("ctx_loaded")
        vec_loaded = sem("vec_loaded")
        ff_loaded = sem("ff_loaded")
        qkv_loaded = [[sem(f"qkv_loaded{l}{b}") for b in range(2)] for l in range(2)]
        wo_loaded = [[sem(f"wo_loaded{l}{b}") for b in range(2)] for l in range(2)]
        consts_set = sem("consts_set")
        ident_zeroed = sem("ident_zeroed")
        ident_ready = sem("ident_ready")
        key_ones = sem("key_ones")
        stats_done = sem("stats_done")
        moments_done = sem("moments_done")
        std_done = sem("std_done")
        rstd_done = sem("rstd_done")
        normalised = sem("normalised")
        xn_turned = sem("xn_turned")
        xn_ready = sem("xn_ready")
        ctx_turned = sem("ctx_turned")
        ctx_ready = sem("ctx_ready")
        bias_added = sem("bias_added")
        scores_ready = [sem(f"scores_ready{l}") for l in range(2)]
        probs_ready = [sem(f"probs_ready{l}") for l in range(2)]
        values_used = [sem(f"values_used{l}") for l in range(2)]
        max_tile_ready = sem("max_tile_ready")
        max_tile_taken = sem("max_tile_taken")
        head_max_ready = sem("head_max_ready")
        work_ready = sem("work_ready")
        work_taken = [sem(f"work_taken{n}") for n in range(2)]
        queries_doubled = sem("queries_doubled")
        keys_doubled = sem("keys_doubled")
        rows_placed = [sem(f"rows_placed{a}") for a in range(2)]
        hi_ready = sem("hi_ready")
        sums_added = [sem(f"sums_added{l}") for l in range(2)]
        out_copied = sem("out_copied")
        out_normed = sem("out_normed")
        gate_ready = sem("gate_ready")
        up_ready = sem("up_ready")
        gelu_done = sem("gelu_done")
        hidden_done = sem("hidden_done")
        down_ready = sem("down_ready")
        result_ready = sem("result_ready")
        out_stored = sem("out_stored")

        QKV_DMAS = [3, 5]

        def job_bank(unit, name):
            number = jobs.numbers[unit.layer, unit.u, name]
            return four_banks[number % 4] if unit.u < 0 and name[0] != "r" else work_banks[number % 2]

        def wait_taken(eng, unit, name, back=0):
            parity, value = jobs.taken(unit, name, back)
            wait(eng, work_taken[parity], value)

        def taken(unit, name):
            return work_taken[jobs.taken(unit, name)[0]]

        block = ctx.enter_context(nc.Block())

        @block.sync
        def _(sp):
            def load_qkv(l, b, cols):
                s = qkv_loaded[l][b]
                sp.dma_start(w_q[l][b][:, :, :], wq_dram[l][:, :, cols]).then_inc(s, 16)
                for w, dram in ((w_k, (Wk1, Wk2)[l]), (w_v, (Wv1, Wv2)[l])):
                    if l == 0:
                        sp.dma_start(w[l][b][:, :, :],
                                     dram.rearrange("(c p) n -> p c n", p=P)[:, :, cols]).then_inc(s, 16)
                    else:
                        for c, rows in enumerate(cross_attn.key_rows):
                            sp.dma_start(w[l][b][0:rows, c, :], dram[c * P:c * P + rows, cols]).then_inc(s, 16)

            for g in range(4):
                sp.dma_start(x_sb[:, 4 * g:4 * g + 4, :], x_dram[:, 4 * g:4 * g + 4, :]).then_inc(x_loaded[g], 16)
            for n, (g, b) in enumerate(((g1, b1), (g2, b2), (g3, b3))):
                sp.dma_start(gains[:, n, :], g.rearrange("(c p) -> p c", p=P), allow_slow_non_contiguous=True).then_inc(vec_loaded, 16)
                sp.dma_start(shifts[:, n, :], b.rearrange("(c p) -> p c", p=P), allow_slow_non_contiguous=True).then_inc(vec_loaded, 16)
            for n, b in enumerate((bo1, bo2, bf)):
                sp.dma_start(bias_b[:, n, :], b.partition_broadcast(P)).then_inc(vec_loaded, 16)
            sp.dma_start(bp_sb[:, :], bp.rearrange("(f p) -> p f", p=P), allow_slow_non_contiguous=True).then_inc(vec_loaded, 16)
            load_qkv(0, 0, slice(0, P))
            full = (CTX_TILES - 1) * P
            sp.dma_start(ctx_stage[:, 0:CTX_TILES - 1, :],
                         ctx_rows[0:full, :].rearrange("(t p) d -> p t d", p=P)).then_inc(ctx_loaded, 16)
            sp.dma_start(ctx_stage[0:CTX_LAST, CTX_TILES - 1, :], ctx_rows[full:CTX_TOKENS, :]).then_inc(ctx_loaded, 16)
            load_qkv(0, 1, slice(P, 2 * P))
            for l in range(2):
                for b in range(2):
                    sp.dma_start(w_o[l][b][:, :], wo_dram[l][:, b, :]).then_inc(wo_loaded[l][b], 16)
            for b in range(2):
                load_qkv(1, b, slice(b * P, b * P + P))
            def attention(l, A):
                def job(unit, name):
                    nxt = unit.next
                    if name == "q":
                        sp.wait_ge(hi_ready, jobs.split(unit, name) + 1)
                        for a in range(2):
                            q = q_hi[nxt % 2][a]
                            sp.dma_start(q[HALF:P, :].bitcast(FP32), q[0:HALF, :].bitcast(FP32)).then_inc(queries_doubled, 16)
                    elif name[0] == "k":
                        sp.wait_ge(hi_ready, jobs.split(unit, name) + 1)
                        start, width = layers[unit.next_pair_layer].key_chunks[int(name[1])]
                        b = unit.next_pair % 2
                        for a in range(2):
                            sp.dma_start(k_hi_one[b][a][0:HALF, start:start + width].bitcast(FP32),
                                         k_hi_lo[b][a][0:HALF, start:start + width].bitcast(FP32)).then_inc(keys_doubled, 16)
                    elif name[:3] == "row":
                        a = int(name[3])
                        wait_taken(sp, unit, name)
                        for i in range(Q_TILES):
                            sp.dma_start(q_lo[nxt % 2][a][HALF:HALF + 1, i * P:(i + 1) * P].bitcast(FP32),
                                         max_rows[a][i:i + 1, :].bitcast(FP32)).then_inc(rows_placed[a], 16)

                if l == 0:
                    for name in FIRST_JOBS:
                        job(Unit(0, -1), name)
                for unit in units(sp, l):
                    if l == 1 and unit.u == UNITS - CHUNKS:
                        sp.wait_ge(scores_ready[1], 2 * unit.u * A.steps)
                        sp.dma_start(w_p[:, :, :], Wp.rearrange("(c p) n -> p c n", p=P)).then_inc(ff_loaded, 16)
                        sp.dma_start(w_f[:, :, :], Wf.rearrange("(f p) n -> p f n", p=P)).then_inc(ff_loaded, 16)
                    for t in range(A.steps):
                        for name in A.jobs_at(unit, t):
                            job(unit, name)
                            if name == "q" and unit.chunk == 2 and unit.u // CHUNKS + 2 < PAIRS:
                                sp.wait_ge(work_ready, jobs.number(unit, "q") + 1)
                                b = unit.pair_parity
                                load_qkv(l, b, bass.ds(unit.at((unit.u // CHUNKS + 2) * P, 2 * P), P))
                            if name == "y1" and unit.chunk == 0 and CHUNKS <= unit.u < UNITS - CHUNKS:
                                sp.wait_ge(work_ready, jobs.number(unit, "y1") + 1)
                                pair = unit.u // CHUNKS + 1
                                sp.dma_start(w_o[l][pair % 2][:, :], wo_dram[l][:, bass.ds(unit.at(pair, 2), 1), :]
                                             .rearrange("p r n -> p (r n)")).then_inc(wo_loaded[l][pair % 2], 16)

            for l, A in enumerate(layers):
                attention(l, A)
            with sp.Fori(0, CHUNKS) as q:
                sp.wait_ge(result_ready, q * 2 + 2)
                sp.dma_start(out_dram[:, bass.ds(q * 4, 4), :], x_sb[:, bass.ds(q * 4, 4), :]).then_inc(out_stored, 16)
            sp.wait_ge(out_stored, 16 * CHUNKS)

        @block.gpsimd
        def _(pool):
            nc.gpsimd.memset(ident[:, :], 0.0).then_inc(ident_zeroed, 1)
            pool.wait_ge(ident_zeroed, 1)
            nc.gpsimd.affine_select(out=ident[:, :], in_=ident[:, :], compare_op=ALU.not_equal, fill=1.0,
                                    base=0, pattern=[[-1, P]], channel_multiplier=1).then_inc(ident_ready, 1)

            def attention(l, A):
                for unit in units(pool, l):
                    for s in range(1, A.steps):
                        if s in A.dve_adds:
                            continue
                        rows = A.tile_keys[s]
                        acc = sums[0:rows, unit.parity, :, :]
                        first = probs[0:rows, unit.u * A.steps % RING, :, :] if s == 1 else acc
                        if s == 1 and not unit.first:
                            pool.wait_ge(work_ready, jobs.sums_read(unit))
                        if s > 1:
                            pool.wait_ge(sums_added[l], A.added(unit, s - 1))
                        pool.wait_ge(probs_ready[l], unit.at(2 * (unit.u * A.steps + s) + 2, 2 * PERIOD * A.steps))
                        nc.gpsimd.tensor_tensor(acc, first, probs[0:rows, (unit.u * A.steps + s) % RING, :, :],
                                                ALU.add).then_inc(sums_added[l], 1)

            attention(0, self_attn)
            attention(1, cross_attn)

        @block.tensor
        def _(pe):
            def first_norm():
                pe.wait_ge(ident_ready, 1)
                for g in range(4):
                    for c in range(DIM_TILES):
                        k = 2 * g + c
                        wait(pe, xn_ready, k - 3)
                        for j in range(4):
                            pe.wait_ge(normalised, 4 * g + j + 1)
                            last = nc.tensor.transpose(four_banks[k % 4][:, j * P:(j + 1) * P],
                                                       xn_stage[:, 4 * g + j, c * P:(c + 1) * P], ident[:, :])
                        last.then_inc(xn_turned, 1)

            def turn_context():
                pe.wait_ge(ctx_loaded, 32)
                for g in range(4):
                    for c, rows in enumerate(cross_attn.key_rows):
                        k = 2 * g + c
                        pe.wait_ge(xn_ready, 8)
                        wait(pe, ctx_ready, k - 3)
                        for t in range(4 * g, min(4 * g + 4, CTX_TILES)):
                            m = cross_attn.tile_keys[t]
                            last = nc.tensor.transpose(
                                four_banks[k % 4][0:rows, (t - 4 * g) * P:(t - 4 * g) * P + m],
                                ctx_stage[0:m, t, c * P:c * P + rows], ident[0:m, 0:m])
                        last.then_inc(ctx_turned, 1)

            def attention(l, A):
                def scores(unit, t):
                    m = A.tile_keys[t]
                    cols = slice(t * P, t * P + m)
                    for a in range(2):
                        k_both, k_one = k_hi_lo[unit.pair_parity][a], k_hi_one[unit.pair_parity][a]
                        dst = score_banks[a][0:m, :]
                        if l == 1 and unit.u == 0 and t == 0:
                            pe.wait_ge(probs_ready[0], 2 * (UNITS * self_attn.steps - 1) + a + 1)
                        elif not (unit.first and t == 0):
                            pe.wait_ge(probs_ready[l], unit.at(2 * (unit.u * A.steps + t - 1) + a + 1,
                                                               2 * PERIOD * A.steps))
                        nc.tensor.matmul(dst, k_both[:, cols], q_hi[unit.parity][a][:, :], start=True, stop=False)
                        if t == 0:
                            pe.wait_ge(rows_placed[a], unit.at(64 * (unit.overall + 1), 64 * PERIOD))
                            if unit.chunk == 0 and a == 0:
                                pe.wait_ge(keys_doubled, unit.at(128 * (unit.overall // CHUNKS + 1), 256))
                        nc.tensor.matmul(dst, k_one[:, cols], q_lo[unit.parity][a][:, :],
                                         start=False, stop=True).then_inc(scores_ready[l], 1)
                        yield

                def weighted_values(unit, t):
                    m = A.tile_keys[t]
                    slot = (unit.u * A.steps + t) % RING
                    pe.wait_ge(probs_ready[l], unit.at(2 * (unit.u * A.steps + t) + 2, 2 * PERIOD * A.steps))
                    if t == 0 and not unit.first:
                        pe.wait_ge(out_copied, unit.at(unit.overall, PERIOD))
                        if unit.chunk == 0:
                            before = Unit(l, unit.u - 1, unit.i) if unit.u > 0 else Unit(0, UNITS - 1)
                            wait_taken(pe, before, "v3")
                    for a in range(2):
                        last = nc.tensor.matmul(out_bank[a * HALF:(a + 1) * HALF, :],
                                                v_sb[0:m, unit.pair_parity, t, a * HALF:(a + 1) * HALF],
                                                probs[0:m, slot, a, :], start=(t == 0), stop=(t == A.steps - 1))
                    last.then_inc(values_used[l], 1)

                def max_tile(unit, n):
                    nxt = unit.next
                    a, i, kc = n // 16, n // 4 % 4, n % 4
                    start, width = layers[unit.next_layer].max_chunks[kc]
                    dst = max_banks[n % 3][:, 0:width]
                    last_in_bank = n - 3 if n > 2 else MAX_TILES - 1 - (MAX_TILES - 1 - n) % 3 - MAX_TILES
                    if not (unit.u == -1 and n < 3):
                        pe.wait_ge(max_tile_taken, unit.at(MAX_TILES * (unit.overall + 1) + last_in_bank + 1, PERIOD * MAX_TILES))
                    if n == 0:
                        wait_taken(pe, unit, "q")
                        pe.wait_ge(queries_doubled, unit.at(32 * (unit.overall + 2), 32 * PERIOD))
                    nc.tensor.matmul(dst, q_hi[nxt % 2][a][:, i * P:(i + 1) * P],
                                     k_hi_lo[(nxt // CHUNKS) % 2][a][:, start:start + width],
                                     start=True, stop=True).then_inc(max_tile_ready, 1)

                def job(unit, name):
                    work = job_bank(unit, name)
                    wait_taken(pe, unit, name, 4 if unit.u < 0 and name[0] in "kq" else 2)
                    nxt, pair = unit.next, unit.next_pair
                    B = layers[unit.next_pair_layer]
                    src = (xn_t, ctx_t)[B.layer]
                    if name == "q":
                        chunk = nxt % CHUNKS
                        for c in range(DIM_TILES):
                            last = nc.tensor.matmul(work[:, :], w_q[unit.next_layer][(nxt // CHUNKS) % 2][:, c, :],
                                                    xn_t[:, c, chunk * BANK:(chunk + 1) * BANK],
                                                    start=(c == 0), stop=(c == DIM_TILES - 1))
                    elif name[0] == "k":
                        if name == "k0":
                            pe.wait_ge(qkv_loaded[B.layer][pair % 2],
                                       unit.at(16 * QKV_DMAS[B.layer] * (pair // 2 + 1), 16 * QKV_DMAS[B.layer]))
                        start, width = B.key_chunks[int(name[1])]
                        for c, rows in enumerate(B.key_rows):
                            last = nc.tensor.matmul(work[:, 0:width], w_k[B.layer][pair % 2][0:rows, c, :],
                                                    src[0:rows, c, start:start + width],
                                                    start=(c == 0), stop=(c == DIM_TILES - 1))
                    elif name[0] == "v":
                        for t in range(4 * int(name[1]), min(4 * int(name[1]) + 4, B.steps)):
                            m = B.tile_keys[t]
                            for c, rows in enumerate(B.key_rows):
                                last = nc.tensor.matmul(work[0:m, (t % 4) * P:(t % 4 + 1) * P],
                                                        src[0:rows, c, t * P:t * P + m],
                                                        w_v[B.layer][pair % 2][0:rows, c, :],
                                                        start=(c == 0), stop=(c == DIM_TILES - 1))
                    elif name == "sum":
                        if unit.prev_layer == l:
                            pe.wait_ge(sums_added[l], unit.at(unit.u * A.adds, PERIOD * A.adds))
                        else:
                            pe.wait_ge(sums_added[0], UNITS * self_attn.adds)
                        prev = (unit.u - 1) % 2
                        for a in range(2):
                            last = nc.tensor.matmul(work[a * HALF:(a + 1) * HALF, :], ones[:, 0:HALF],
                                                    sums[:, prev, a, :], start=True, stop=True)
                    elif name[0] == "y":
                        prev_pair = unit.prev_pair
                        if name == "y0":
                            pe.wait_ge(out_normed, unit.at(unit.overall, PERIOD))
                            if (unit.u - 1) % CHUNKS == 0:
                                pe.wait_ge(wo_loaded[l][prev_pair % 2], unit.at(16 * (prev_pair // 2 + 1), 16))
                        for k in range(2):
                            i = 2 * int(name[1]) + k
                            last = nc.tensor.matmul(work[:, k * DIM:(k + 1) * DIM], o_norm[:, i * P:(i + 1) * P],
                                                    w_o[unit.prev_layer][prev_pair % 2][:, :], start=True, stop=True)
                    elif name[:2] == "ln":
                        norm, chunk = unit.norm(int(name[2]) // 2)
                        c = int(name[2]) % 2
                        pe.wait_ge(normalised, TOKEN_TILES * norm + 4 * chunk + 4)
                        for j in range(Q_TILES):
                            last = nc.tensor.transpose(work[:, j * P:(j + 1) * P],
                                                       norm_stage[:, j, c * P:(c + 1) * P], ident[:, :])
                    else:
                        a = int(name[3])
                        pe.wait_ge(head_max_ready, unit.at(2 * (unit.overall + 1) + a + 1, 2 * PERIOD))
                        last = nc.tensor.transpose(work[0:Q_TILES, 0:P],
                                                   query_max[:, a * Q_TILES:(a + 1) * Q_TILES], ident[:, :])
                    last.then_inc(work_ready, 1)

                if l == 0:
                    before = Unit(0, -1)
                    pe.wait_ge(xn_ready, 8)
                    pe.wait_ge(ctx_ready, 8)
                    pe.wait_ge(key_ones, 4)
                    pe.wait_ge(consts_set, 1)
                    for name in ("k0", "k1", "k2", "k3", "q", "v0", "v1", "v2", "v3"):
                        job(before, name)
                    for n in range(MAX_TILES):
                        max_tile(before, n)
                    job(before, "row0")
                    job(before, "row1")
                for unit in units(pe, l):
                    for t in range(A.steps):
                        tiles = list(A.max_at[t]) if unit.has_next else []
                        for _ in scores(unit, t):
                            if tiles and tiles[0] > 0:
                                max_tile(unit, tiles.pop(0))
                        for name in A.jobs_at(unit, t):
                            job(unit, name)
                        if t > 0:
                            weighted_values(unit, t - 1)
                        elif unit.u > 0:
                            weighted_values(Unit(l, unit.u - 1, unit.i), A.steps - 1)
                        for n in tiles:
                            max_tile(unit, n)
                weighted_values(unit, A.steps - 1)
                return job

            first_norm()
            turn_context()
            attention(0, self_attn)
            job = attention(1, cross_attn)
            after = Unit(1, UNITS)
            job(after, "sum")

            pe.wait_ge(ff_loaded, 32)
            pe.wait_ge(max_tile_taken, 2 * UNITS * MAX_TILES)
            pe.wait_ge(probs_ready[1], 2 * UNITS * cross_attn.steps)
            pe.wait_ge(out_copied, 2 * UNITS)

            def feed_forward(q):
                for f in range(FF_TILES):
                    for name in {2: ("y0", "y1"), 5: ("ln0", "ln1")}.get(f, ()) if isinstance(q, int) else ():
                        job(after, name)
                    gate, up = ff_banks[2 * (f % 2)], ff_banks[2 * (f % 2) + 1]
                    wait(pe, hidden_done, q * FF_TILES + (f - 1))
                    for dst, col, s in ((gate, FF + f * P, gate_ready), (up, f * P, up_ready)):
                        for c in range(DIM_TILES):
                            last = nc.tensor.matmul(dst[:, :], w_p[:, c, col:col + P],
                                                    xn_t[:, c, bass.ds(q * BANK, BANK)],
                                                    start=(c == 0), stop=(c == DIM_TILES - 1))
                        last.then_inc(s, 1)
                for j in range(2):
                    wait(pe, result_ready, q * 2 + (j - 1))
                    pe.wait_ge(hidden_done, q * FF_TILES + FF_TILES)
                    for k in range(2):
                        i = 2 * j + k
                        for f in range(FF_TILES):
                            last = nc.tensor.matmul(score_banks[j][:, k * DIM:(k + 1) * DIM],
                                                    hidden[:, f, i * P:(i + 1) * P], w_f[:, f, :],
                                                    start=(f == 0), stop=(f == FF_TILES - 1))
                    last.then_inc(down_ready, 1)

            feed_forward(0)
            for name in ("ln0", "ln1"):
                wait_taken(pe, after, name)
            with pe.Fori(1, CHUNKS) as q:
                feed_forward(q)

        @block.scalar
        def _(act):
            def std_of(n, g):
                act.wait_ge(moments_done, TOKEN_TILES * n + 4 * g + 4)
                nc.scalar.activation(std[:, 4 * g:4 * g + 4], moments[:, 4 * g:4 * g + 4, 1], ACT.Sqrt,
                                     bias=eps_col[:, :]).then_inc(std_done, 1)

            def take_norm(n, g, c, bank, done):
                nc.scalar.activation(xn_t[:, c, g * BANK:(g + 1) * BANK], bank[:, :], ACT.Identity,
                                     bias=shifts[:, n, c:c + 1], scale=gains[:, n, c:c + 1]).then_inc(done, 1)

            def first_norm():
                act.wait_ge(consts_set, 1)
                for g in range(4):
                    std_of(0, g)
                act.wait_ge(vec_loaded, 160)
                for g in range(4):
                    for c in range(DIM_TILES):
                        k = 2 * g + c
                        act.wait_ge(xn_turned, k + 1)
                        take_norm(0, g, c, four_banks[k % 4], xn_ready)

            def take_context():
                for g in range(4):
                    for c, rows in enumerate(cross_attn.key_rows):
                        k = 2 * g + c
                        width = min(BANK, CTX_TOKENS - g * BANK)
                        act.wait_ge(ctx_turned, k + 1)
                        nc.scalar.copy(ctx_t[0:rows, c, g * BANK:g * BANK + width],
                                       four_banks[k % 4][0:rows, 0:width]).then_inc(ctx_ready, 1)

            def attention(l, A):
                def exp(unit, t):
                    m = A.tile_keys[t]
                    slot = (unit.u * A.steps + t) % RING
                    for a in range(2):
                        act.wait_ge(scores_ready[l], unit.at(2 * (unit.u * A.steps + t) + a + 1,
                                                             2 * PERIOD * A.steps))
                        if a == 0 and not (unit.first and t < RING):
                            if t >= RING:
                                act.wait_ge(values_used[l], unit.at(unit.u * A.steps + t - RING + 1, PERIOD * A.steps))
                                act.wait_ge(sums_added[l], A.added(unit, t - RING))
                            else:
                                B = layers[unit.prev_layer]
                                prev = Unit(B.layer, (unit.u - 1) % UNITS, unit.i)
                                act.wait_ge(values_used[B.layer], prev.at(prev.u * B.steps + B.steps + t - RING + 1,
                                                                          PERIOD * B.steps))
                                act.wait_ge(sums_added[B.layer], B.added(prev, B.steps + t - RING))
                        src = score_banks[a][0:m, :]
                        nc.scalar.activation(probs[0:m, slot, a, :], src, ACT.Exp,
                                             scale=SCALE).then_inc(probs_ready[l], 1)

                def job(unit, name):
                    if name[0] not in "qkvrl":
                        return
                    act.wait_ge(work_ready, jobs.number(unit, name) + 1)
                    work = job_bank(unit, name)
                    nxt, pair_parity = unit.next, unit.next_pair % 2
                    B = layers[unit.next_pair_layer]
                    if name == "q":
                        for a in range(2):
                            src = work[a * HALF:(a + 1) * HALF, :]
                            last = nc.scalar.copy(q_hi[nxt % 2][a][0:HALF, :], src)
                        last.then_inc(hi_ready, 1)
                    elif name[0] == "k":
                        start, width = B.key_chunks[int(name[1])]
                        for a in range(2):
                            src = work[a * HALF:(a + 1) * HALF, 0:width]
                            last = nc.scalar.copy(k_hi_lo[pair_parity][a][0:HALF, start:start + width], src)
                        last.then_inc(hi_ready, 1)
                    elif name[0] == "v":
                        t0 = 4 * int(name[1])
                        tiles = min(4, B.steps - t0)
                        m = B.tile_keys[t0]
                        nc.scalar.copy(v_sb[0:m, pair_parity, t0:t0 + tiles, :],
                                       work[0:m, 0:tiles * P].rearrange("p (t n) -> p t n", n=P)
                                       ).then_inc(taken(unit, name), 1)
                    elif name[:2] == "ln":
                        norm, chunk = unit.norm(int(name[2]) // 2)
                        take_norm(norm, chunk, int(name[2]) % 2, work, taken(unit, name))
                    else:
                        nc.scalar.mul(max_rows[int(name[3])][:, :], work[0:Q_TILES, 0:P],
                                      -1.0).then_inc(taken(unit, name), 1)

                def copy_out(unit):
                    if unit.prev_layer == l:
                        act.wait_ge(values_used[l], unit.at(unit.u * A.steps, PERIOD * A.steps))
                    else:
                        act.wait_ge(values_used[0], UNITS * self_attn.steps)
                    nc.scalar.copy(o_raw[:, (unit.u - 1) % 2, :], out_bank[:, :]).then_inc(out_copied, 1)

                if l == 0:
                    for name in FIRST_JOBS:
                        job(Unit(0, -1), name)
                for unit in units(act, l):
                    for t in range(A.steps):
                        exp(unit, t)
                        for half, step in enumerate((1, A.steps - 2)):
                            if t == step and unit.norm(half):
                                std_of(*unit.norm(half))
                        for name in A.jobs_at(unit, t):
                            job(unit, name)
                        if t == 0 and not unit.first:
                            copy_out(unit)
                return job, copy_out

            first_norm()
            take_context()
            act.wait_ge(consts_set, 1)
            for b in range(2):
                for a in range(2):
                    for n in range(TOKENS // BANK):
                        last = nc.scalar.copy(k_hi_one[b][a][HALF:HALF + 1, n * BANK:(n + 1) * BANK], one_row[:, :])
                    last.then_inc(key_ones, 1)
            attention(0, self_attn)
            job, copy_out = attention(1, cross_attn)
            after = Unit(1, UNITS)
            copy_out(after)

            def gelu(q):
                for f in range(FF_TILES):
                    if isinstance(q, int) and f == 3:
                        std_of(*after.norm(0))
                    if isinstance(q, int) and f == 5:
                        job(after, "ln0")
                        job(after, "ln1")
                    wait(act, gate_ready, q * FF_TILES + (f + 1))
                    wait(act, hidden_done, q * FF_TILES + (f - 1))
                    nc.scalar.activation(gelu_sb[:, f % 2, :], ff_banks[2 * (f % 2)][:, :], ACT.Gelu,
                                         bias=bp_sb[:, FF_TILES + f:FF_TILES + f + 1]).then_inc(gelu_done, 1)

            gelu(0)
            with act.Fori(1, CHUNKS) as q:
                gelu(q)

        @block.vector
        def _(dve):
            nc.vector.memset(ones[:, :], 1.0)
            nc.vector.memset(one_row[:, :], 1.0)
            nc.vector.memset(eps_col[:, :], EPS).then_inc(consts_set, 1)

            def token_stats(n, g):
                for t in range(4 * g, 4 * g + 4):
                    nc.vector.bn_stats(stats[:, t, :], x_sb[:, t, :]).then_inc(stats_done, 1)
                for t in range(4 * g, 4 * g + 4):
                    dve.wait_ge(stats_done, TOKEN_TILES * n + t + 1)
                    nc.vector.bn_aggr(moments[:, t, :], stats[:, t, :]).then_inc(moments_done, 1)

            def normalise(n, g, stage):
                dve.wait_ge(std_done, 4 * n + g + 1)
                nc.vector.reciprocal(rstd[:, 4 * g:4 * g + 4], std[:, 4 * g:4 * g + 4]).then_inc(rstd_done, 1)
                dve.wait_ge(rstd_done, 4 * n + g + 1)
                for j in range(4):
                    t = 4 * g + j
                    nc.vector.tensor_scalar(stage[:, j, :], x_sb[:, t, :], moments[:, t, 0:1],
                                            rstd[:, t:t + 1], ALU.subtract, ALU.mult).then_inc(normalised, 1)

            def add_bias(n, g):
                dve.wait_ge(normalised, TOKEN_TILES * n + 4 * g + 4)
                rows = x_sb[:, 4 * g:4 * g + 4, :]
                nc.vector.tensor_tensor(rows, rows, bias_b[:, n:n + 1, :].to_broadcast([P, 4, DIM]),
                                        ALU.add).then_inc(bias_added, 1)

            def first_norm():
                for g in range(4):
                    dve.wait_ge(x_loaded[g], 16)
                    token_stats(0, g)
                for g in range(4):
                    normalise(0, g, xn_stage[:, 4 * g:4 * g + 4, :])
                dve.wait_ge(vec_loaded, 160)
                for g in range(4):
                    add_bias(0, g)

            def later_stats(unit, half):
                n, g = unit.norm(half)
                from_unit = unit if half == 1 or unit.u == UNITS else Unit(*((unit.layer, unit.u - 1) if unit.u > 0
                                                                             else (0, UNITS - 1)))
                wait_taken(dve, from_unit, "y1")
                token_stats(n, g)

            def later_norm(unit, half):
                n, g = unit.norm(half)
                if (n, g) != (1, 0):
                    dve.wait_ge(work_ready, jobs.last_turned(unit, half))
                normalise(n, g, norm_stage)
                add_bias(n, g)

            def attention(l, A):
                def take_max(unit, n):
                    nxt = unit.overall + 1
                    a, j, kc = n // 16, n // 4, n % 4
                    width = layers[unit.next_layer].max_chunks[kc][1]
                    dve.wait_ge(max_tile_ready, unit.at(MAX_TILES * nxt + n + 1, PERIOD * MAX_TILES))
                    nc.vector.tensor_reduce(part_max[:, j, kc:kc + 1], max_banks[n % 3][:, 0:width], AX.X,
                                            ALU.max).then_inc(max_tile_taken, 1)
                    if n % 16 == 15:
                        dve.wait_ge(max_tile_taken, unit.at(MAX_TILES * nxt + n + 1, PERIOD * MAX_TILES))
                        heads = slice(a * Q_TILES, (a + 1) * Q_TILES)
                        nc.vector.tensor_reduce(query_max[:, heads], part_max[:, heads, :], AX.X,
                                                ALU.max).then_inc(head_max_ready, 1)

                def add_probs(unit, s):
                    rows = A.tile_keys[s]
                    acc = sums[0:rows, unit.parity, :, :]
                    dve.wait_ge(probs_ready[l], unit.at(2 * (unit.u * A.steps + s) + 2, 2 * PERIOD * A.steps))
                    dve.wait_ge(sums_added[l], A.added(unit, s - 1))
                    nc.vector.tensor_tensor(acc, acc, probs[0:rows, (unit.u * A.steps + s) % RING, :, :],
                                            ALU.add).then_inc(sums_added[l], 1)

                def job(unit, name):
                    nxt = unit.next
                    work = job_bank(unit, name)
                    if name[0] in "qk":
                        pair_parity = unit.next_pair % 2
                        dve.wait_ge(hi_ready, jobs.split(unit, name) + 1)
                        for a in range(2):
                            if name == "q":
                                hi = q_hi[nxt % 2][a][0:HALF, :]
                                lo, width = q_lo[nxt % 2][a][0:HALF, :], BANK
                            else:
                                start, width = layers[unit.next_pair_layer].key_chunks[int(name[1])]
                                both = k_hi_lo[pair_parity][a]
                                hi, lo = both[0:HALF, start:start + width], both[HALF:P, start:start + width]
                            last = nc.vector.tensor_tensor(lo, work[a * HALF:(a + 1) * HALF, 0:width],
                                                           hi.bitcast(FP32), ALU.subtract)
                        last.then_inc(taken(unit, name), 1)
                    elif name == "sum":
                        dve.wait_ge(work_ready, jobs.number(unit, name) + 1)
                        for part in range(4):
                            cols = slice(part * P, (part + 1) * P)
                            last = nc.vector.reciprocal(sum_recip[:, cols], work[:, cols])
                            if part < 3:
                                yield
                        last.then_inc(taken(unit, name), 1)
                        wait_taken(dve, unit, name)
                        dve.wait_ge(out_copied, unit.at(unit.overall, PERIOD))
                        nc.vector.tensor_tensor(o_norm[:, :], o_raw[:, (unit.u - 1) % 2, :], sum_recip[:, :],
                                                ALU.mult).then_inc(out_normed, 1)
                    elif name[0] == "y":
                        t = 4 * ((unit.u - 1) % CHUNKS) + 2 * int(name[1])
                        rows = x_sb[:, t:t + 2, :]
                        dve.wait_ge(work_ready, jobs.number(unit, name) + 1)
                        nc.vector.tensor_tensor(rows, rows, work[:, :].rearrange("p (t d) -> p t d", d=DIM),
                                                ALU.add).then_inc(taken(unit, name), 1)

                def finish(parts):
                    for _ in parts:
                        pass

                if l == 0:
                    before = Unit(0, -1)
                    for name in ("k0", "k1", "k2", "k3", "q"):
                        finish(job(before, name))
                    for n in range(MAX_TILES):
                        take_max(before, n)
                late_job = None
                for unit in units(dve, l):
                    if unit.u == 1:
                        dve.wait_ge(bias_added, 4 * l + 4)
                    for t in range(A.steps):
                        tiles = list(A.max_at[t]) if unit.has_next else []
                        for half, step in enumerate((1, A.steps - 2)):
                            if unit.norm(half) and t == step:
                                later_stats(unit, half)
                                if half == 0:
                                    later_norm(unit, half)
                            if unit.norm(half) and half == 1 and t == step + 1:
                                later_norm(unit, half)
                        if late_job:
                            finish(late_job)
                            late_job = None
                        for _ in range(A.recips_at(unit, t)):
                            next(recips, None)
                        for n in tiles:
                            take_max(unit, n)
                        for name in A.jobs_at(unit, t):
                            if name[0] == "k" and t < A.steps - 1:
                                late_job = job(unit, name)
                                continue
                            if name == "sum":
                                recips = job(unit, name)
                            else:
                                finish(job(unit, name))
                        if t - 1 in A.dve_adds:
                            add_probs(unit, t - 1)
                return job

            first_norm()
            attention(0, self_attn)
            job = attention(1, cross_attn)
            after = Unit(1, UNITS)
            for _ in job(after, "sum"):
                pass

            def feed_forward(q):
                for f in range(FF_TILES):
                    if isinstance(q, int) and f == 2:
                        for name in ("y0", "y1"):
                            list(job(after, name))
                        later_stats(after, 0)
                    if isinstance(q, int) and f == 3:
                        later_norm(after, 0)
                    dve.wait_ge(up_ready, q * FF_TILES + (f + 1))
                    dve.wait_ge(gelu_done, q * FF_TILES + (f + 1))
                    wait(dve, down_ready, q * 2)
                    nc.vector.scalar_tensor_tensor(hidden[:, f, :], ff_banks[2 * (f % 2) + 1][:, :],
                                                   bp_sb[:, f:f + 1], gelu_sb[:, f % 2, :], ALU.add,
                                                   ALU.mult).then_inc(hidden_done, 1)
                for j in range(2):
                    dve.wait_ge(down_ready, q * 2 + (j + 1))
                    if isinstance(q, int):
                        dve.wait_ge(bias_added, 12)
                    rows = x_sb[:, bass.ds(q * 4 + 2 * j, 2), :]
                    nc.vector.tensor_tensor(rows, rows, score_banks[j][:, :].rearrange("p (t d) -> p t d", d=DIM),
                                            ALU.add).then_inc(result_ready, 1)

            feed_forward(0)
            with dve.Fori(1, CHUNKS) as q:
                feed_forward(q)


_PREFIX = "L0_xattn_"
_NAMES = ["Wq1", "Wk1", "Wv1", "Wo1", "bo1", "Wq2", "Wk2", "Wv2", "Wo2", "bo2", "Wp", "bp", "Wf", "bf",
          "g1", "b1", "g2", "b2", "g3", "b3"]
_INS = ["x", "ctx_768"] + [_PREFIX + n for n in _NAMES]


def kernel(**inputs):
    import numpy as _np
    import concourse.bacc as _bacc
    from concourse import mybir as _mybir
    from concourse.bass_utils import run_bass_kernel_spmd as _run

    nc = _bacc.Bacc("TRN2", target_bir_lowering=False, num_devices=1)
    arrays, args = {}, []
    for name in _INS:
        a = _np.ascontiguousarray(inputs[name])
        arrays[f"in_{name}_dram"] = a
        args.append(nc.dram_tensor(f"in_{name}_dram", a.shape, _mybir.dt.from_np(a.dtype), kind="ExternalInput").ap())
    out = nc.dram_tensor("out_dram", (1, TOKENS, DIM), _mybir.dt.float32, kind="ExternalOutput").ap()
    xattn_block(nc, *args, out)
    r = _run(nc, [arrays], core_ids=[0])
    return r.results[0]["out_dram"]
```

```python
from contextlib import ExitStack

import concourse.bass as bass
from concourse import mybir

FP32 = mybir.dt.float32
FP32R = mybir.dt.float32r
ALU = mybir.AluOpType
ACT = mybir.ActivationFunctionType
AX = mybir.AxisListType

P = 128
HALF = P // 2
BANK = 512
TOKENS, DIM, CTX_TOKENS, CTX_DIM = 2048, 256, 1601, 192
HEADS, HEAD_DIM = 16, 64
INNER = HEADS * HEAD_DIM
FF = 1024
EPS = 1e-5
SCALE = HEAD_DIM ** -0.5
DIM_TILES = DIM // P
TOKEN_TILES = TOKENS // P
CHUNKS = TOKENS // BANK
PAIRS = HEADS // 2
UNITS = PAIRS * CHUNKS
PERIOD = 2 * CHUNKS
Q_TILES = BANK // P
MAX_TILES = 2 * Q_TILES * 4
RING = 4
CTX_TILES = -(-CTX_TOKENS // P)
CTX_LAST = CTX_TOKENS - (CTX_TILES - 1) * P
FF_TILES = FF // P


class Unit:

    def __init__(self, layer, u, i=None):
        self.layer, self.u, self.i = layer, u, i
        self.overall = layer * UNITS + u
        self.chunk = u % CHUNKS
        self.parity = u % 2
        self.pair_parity = (u // CHUNKS) % 2
        self.first = layer == 0 and u == 0
        ahead = i is not None or layer == 0
        self.has_next = ahead or u < UNITS - 1
        self.has_next_pair = ahead or u < UNITS - CHUNKS
        self.next_layer = min(layer + (u == UNITS - 1), 1)
        self.next_pair_layer = min(layer + (u >= UNITS - CHUNKS), 1)
        self.next = (u + 1) % UNITS
        self.next_pair = (u // CHUNKS + 1) % PAIRS
        self.prev_layer = layer - (u == 0)
        self.prev_pair = ((u - 1) // CHUNKS) % PAIRS

    def at(self, value, per_period):
        return value if self.i is None else self.i * per_period + value

    def norm(self, half):
        if self.i is None:
            return {(0, 30, 0): (1, 0), (0, 31, 0): (1, 1), (1, 0, 0): (1, 2), (1, 0, 1): (1, 3),
                    (1, 30, 0): (2, 0), (1, 31, 0): (2, 1), (1, 31, 1): (2, 2), (1, 32, 0): (2, 3),
                    }.get((self.layer, self.u, half))


def units(eng, layer):
    yield Unit(layer, 0)
    loops = (UNITS - 1) // PERIOD
    with eng.Fori(0, loops) as i:
        for u in range(1, PERIOD + 1):
            yield Unit(layer, u, i)
    for u in range(1 + loops * PERIOD, UNITS):
        yield Unit(layer, u)


class Attention:

    def __init__(self, layer, keys, key_chunks, max_chunks, key_rows, slots, recip_steps, max_steps,
                 norm_slots=None, norm_recip_steps=None):
        self.layer = layer
        self.steps = -(-keys // P)
        self.tile_keys = [min(P, keys - t * P) for t in range(self.steps)]
        self.key_chunks = key_chunks
        self.max_chunks = max_chunks
        self.key_rows = key_rows
        self.slots = slots
        self.recip_steps = recip_steps
        self.norm_slots, self.norm_recip_steps = norm_slots or slots, norm_recip_steps or recip_steps
        assert sum(max_steps) == MAX_TILES and len(max_steps) == self.steps
        self.max_at = [list(range(sum(max_steps[:t]), sum(max_steps[:t + 1]))) for t in range(self.steps)]
        self.adds = self.steps - 1

    def jobs_at(self, unit, t):
        names = []
        for slot, name in self.norm_slots if unit.norm(1) else self.slots:
            if slot == t:
                if name in ("q", "row0", "row1") and not unit.has_next:
                    continue
                if name in ("kv0", "kv1"):
                    if not unit.has_next_pair:
                        continue
                    which = 2 * (unit.chunk % 2) + int(name[2])
                    name = ("k" if unit.chunk < 2 else "v") + str(which)
                if name in ("sum", "y0", "y1") and unit.first:
                    continue
                if name[:2] == "ln" and not unit.norm(int(name[2]) // 2):
                    continue
                names.append(name)
        return names

    def recips_at(self, unit, t):
        steps = self.norm_recip_steps if unit.norm(1) else self.recip_steps
        return 0 if unit.first else steps.count(t)

    def added(self, unit, t):
        return unit.at(unit.u * self.adds + max(t, 1), PERIOD * self.adds)


FIRST_JOBS = ["k0", "k1", "k2", "k3", "q", "v0", "v1", "v2", "v3", "row0", "row1"]
LAST_JOBS = ["sum", "y0", "y1", "ln0", "ln1"]


class Jobs:

    def __init__(self, layers):
        order = [(0, -1, name) for name in FIRST_JOBS]
        for A in layers:
            for u in range(UNITS):
                for t in range(A.steps):
                    order += [(A.layer, u, name) for name in A.jobs_at(Unit(A.layer, u), t)]
        order += [(1, UNITS, name) for name in LAST_JOBS]
        self.numbers = {job: n for n, job in enumerate(order)}
        self.per_period = [self.numbers[l, PERIOD + 1, "q"] - self.numbers[l, 1, "q"] for l in range(2)]
        self.splits = {job: sum(1 for j in order[:n] if j[2][0] in "qk") for n, job in enumerate(order)}

    def number(self, unit, name):
        return unit.at(self.numbers[unit.layer, unit.u, name], self.per_period[unit.layer])

    def taken(self, unit, name, back=0):
        n = self.numbers[unit.layer, unit.u, name] - back
        return n % 2, unit.at(n // 2 + 1, self.per_period[unit.layer] // 2)

    def split(self, unit, name):
        return unit.at(self.splits[unit.layer, unit.u, name], PERIOD + 8)

    def last_turned(self, unit, half):
        turns = [n + 1 for job, n in self.numbers.items() if job[2] in ("ln1", "ln3")]
        number = self.numbers[unit.layer, unit.u, f"ln{2 * half}"]
        return max(n for n in turns if n <= number)

    def sums_read(self, unit):
        per_period = self.per_period[unit.layer]
        if unit.i is None:
            layer, u = (unit.layer, unit.u - 1) if unit.u > 0 else (0, UNITS - 1)
            return self.numbers[layer, u, "sum"] + 1
        if unit.u > 1:
            return unit.at(self.numbers[unit.layer, unit.u - 1, "sum"] + 1, per_period)
        return unit.at(self.numbers[unit.layer, PERIOD, "sum"] + 1 - per_period, per_period)


def wait(eng, sem, value):
    if not isinstance(value, int) or value > 0:
        eng.wait_ge(sem, value)


def xattn_block(nc, x, ctx_768, Wq1, Wk1, Wv1, Wo1, bo1, Wq2, Wk2, Wv2, Wo2, bo2, Wp, bp, Wf, bf,
                g1, b1, g2, b2, g3, b3, out):
    self_attn = Attention(
        0, TOKENS, [(BANK * j, BANK) for j in range(4)], [(BANK * j, BANK) for j in range(4)], [P, P],
        slots=[(0, "q"), (1, "kv0"), (5, "kv1"), (7, "ln0"), (7, "ln1"), (8, "row0"), (8, "sum"),
               (13, "row1"), (14, "y0"), (15, "y1")],
        recip_steps=[9, 10, 12, 13],
        max_steps=[0, 0, 3, 3, 3, 3, 3, 3, 3, 3, 3, 3, 2, 0, 0, 0])
    width = -(-CTX_TOKENS // 8) * 2
    cross_attn = Attention(
        1, CTX_TOKENS, [(BANK * j, min(BANK, CTX_TOKENS - BANK * j)) for j in range(4)],
        [(min(j * (width - 2), CTX_TOKENS - width), width) for j in range(4)], [P, CTX_DIM - P],
        slots=[(0, "q"), (1, "kv0"), (6, "ln0"), (6, "ln1"), (7, "row0"), (7, "sum"),
               (11, "row1"), (12, "y0"), (12, "y1"), (12, "kv1")],
        recip_steps=[8, 9, 10, 11],
        max_steps=[0, 0, 3, 4, 4, 4, 4, 4, 4, 4, 1, 0, 0],
        norm_slots=[(0, "q"), (2, "kv0"), (3, "sum"), (7, "ln0"), (7, "ln1"), (8, "y0"), (9, "y1"),
                    (10, "row0"), (11, "row1"), (12, "kv1"), (12, "ln2"), (12, "ln3")],
        norm_recip_steps=[4, 5, 5, 6])
    assert cross_attn.max_chunks[-1][0] + width == CTX_TOKENS
    layers = [self_attn, cross_attn]
    jobs = Jobs(layers)

    x_dram = x.rearrange("b (t p) d -> p (b t) d", p=P)
    out_dram = out.rearrange("b (t p) d -> p (b t) d", p=P)
    ctx_rows = ctx_768.rearrange("b t d -> (b t) d")
    wq_dram = [w.rearrange("(c p) n -> p c n", p=P) for w in (Wq1, Wq2)]
    wo_dram = [w.rearrange("(r p) n -> p r n", p=P) for w in (Wo1, Wo2)]

    ctx = ExitStack()
    with ctx:
        def sb(name, shape, dtype=FP32, stack=ctx):
            return stack.enter_context(nc.sbuf_tensor(name, shape, dtype))

        def sem(name):
            return ctx.enter_context(nc.semaphore(name))

        x_sb = sb("x_sb", [P, TOKEN_TILES, DIM])
        xn_t = sb("xn_t", [P, DIM_TILES, TOKENS])
        ctx_t = sb("ctx_t", [P, 2, CTX_TOKENS])
        q_hi = [[sb(f"q_hi{b}{a}", [P, BANK], FP32R) for a in range(2)] for b in range(2)]
        q_lo = [[sb(f"q_lo{b}{a}", [HALF + 1, BANK], FP32R) for a in range(2)] for b in range(2)]
        v_sb = sb("v_sb", [P, 2, TOKEN_TILES, P])
        probs = sb("probs", [P, RING, 2, BANK])
        sums = sb("sums", [P, 2, 2, BANK])
        w_q = [[sb(f"w_q{l}{b}", [P, DIM_TILES, P]) for b in range(2)] for l in range(2)]
        w_k = [[sb(f"w_k{l}{b}", [P, DIM_TILES, P]) for b in range(2)] for l in range(2)]
        w_v = [[sb(f"w_v{l}{b}", [P, DIM_TILES, P]) for b in range(2)] for l in range(2)]
        w_o = [[sb(f"w_o{l}{b}", [P, DIM]) for b in range(2)] for l in range(2)]
        o_raw = sb("o_raw", [P, 2, BANK])
        o_norm = sb("o_norm", [P, BANK])
        sum_recip = sb("sum_recip", [P, BANK])
        part_max = sb("part_max", [P, 2 * Q_TILES, 4])
        query_max = sb("query_max", [P, 2 * Q_TILES])
        max_rows = [sb(f"max_rows{a}", [Q_TILES, P], FP32R) for a in range(2)]
        ident = sb("ident", [P, P])
        ones = sb("ones", [P, P])
        one_row = sb("one_row", [1, BANK])
        eps_col = sb("eps_col", [P, 1])
        gains = sb("gains", [P, 3, DIM_TILES])
        shifts = sb("shifts", [P, 3, DIM_TILES])
        bias_b = sb("bias_b", [P, 3, DIM])
        bp_sb = sb("bp_sb", [P, 2 * FF_TILES])
        norm_stage = sb("norm_stage", [P, Q_TILES, DIM])
        stats = sb("stats", [P, TOKEN_TILES, 6])
        moments = sb("moments", [P, TOKEN_TILES, 2])
        std = sb("std", [P, TOKEN_TILES])
        rstd = sb("rstd", [P, TOKEN_TILES])
        attn_memory = ExitStack()
        k_hi_lo, k_hi_one = [], []
        for b in range(2):
            k_hi_lo.append([sb(f"k_hi_lo{b}{a}", [P, TOKENS], FP32R, attn_memory) for a in range(2)])
            k_hi_one.append([sb(f"k_hi_one{b}{a}", [HALF + 1, TOKENS], FP32R, attn_memory) for a in range(2)])
        attn_memory.close()
        w_p = sb("w_p", [P, DIM_TILES, 2 * FF])
        w_f = sb("w_f", [P, FF_TILES, DIM])
        gelu_sb = sb("gelu_sb", [P, 4, BANK])
        hidden = sb("hidden", [P, FF_TILES, BANK])

        xn_stage = probs[:, :, :, :].rearrange("p r a n -> p (r a n)").rearrange("p (t d) -> p t d", d=DIM)
        v_place = v_sb[:, 1, :, :].rearrange("p t n -> p (t n)")
        norm_place = norm_stage[:, :, :].rearrange("p t d -> p (t d)")
        STAGED = TOKENS // CTX_DIM
        ctx_stage = [place[:, 0:n * CTX_DIM].rearrange("p (t d) -> p t d", d=CTX_DIM)
                     for place, n in ((v_place, STAGED), (norm_place, CTX_TILES - STAGED))]

        def ctx_tile(t):
            return ctx_stage[t // STAGED][:, t % STAGED, :]

        def bank(name):
            return ctx.enter_context(nc.psum_tensor(name, [P, BANK], FP32))

        score_banks = [bank(f"scores{n}") for n in range(2)]
        max_banks = [bank(f"max_scores{n}") for n in range(3)]
        out_bank = bank("attn_out")
        work_banks = [bank(f"work{n}") for n in range(2)]
        four_banks = work_banks + score_banks
        ff_banks = max_banks + [out_bank]

        x_loaded = [sem(f"x_loaded{g}") for g in range(4)]
        ctx_loaded = sem("ctx_loaded")
        vec_loaded = sem("vec_loaded")
        ff_loaded = sem("ff_loaded")
        qkv_loaded = [[sem(f"qkv_loaded{l}{b}") for b in range(2)] for l in range(2)]
        wo_loaded = [[sem(f"wo_loaded{l}{b}") for b in range(2)] for l in range(2)]
        consts_set = sem("consts_set")
        ident_zeroed = sem("ident_zeroed")
        ident_ready = sem("ident_ready")
        key_ones = sem("key_ones")
        stats_done = sem("stats_done")
        moments_done = sem("moments_done")
        std_done = sem("std_done")
        rstd_done = sem("rstd_done")
        normalised = sem("normalised")
        xn_turned = sem("xn_turned")
        xn_ready = sem("xn_ready")
        ctx_turned = sem("ctx_turned")
        ctx_ready = sem("ctx_ready")
        bias_added = sem("bias_added")
        scores_ready = [sem(f"scores_ready{l}") for l in range(2)]
        probs_ready = [sem(f"probs_ready{l}") for l in range(2)]
        values_used = [sem(f"values_used{l}") for l in range(2)]
        max_tile_ready = sem("max_tile_ready")
        max_tile_taken = sem("max_tile_taken")
        head_max_ready = sem("head_max_ready")
        work_ready = sem("work_ready")
        work_taken = [sem(f"work_taken{n}") for n in range(2)]
        queries_doubled = sem("queries_doubled")
        keys_doubled = sem("keys_doubled")
        rows_placed = [sem(f"rows_placed{a}") for a in range(2)]
        hi_ready = sem("hi_ready")
        sums_added = [sem(f"sums_added{l}") for l in range(2)]
        out_copied = sem("out_copied")
        out_normed = sem("out_normed")
        gate_ready = sem("gate_ready")
        up_ready = sem("up_ready")
        gelu_done = sem("gelu_done")
        hidden_done = sem("hidden_done")
        down_ready = sem("down_ready")
        result_ready = sem("result_ready")
        out_stored = sem("out_stored")

        QKV_DMAS = [3, 5]

        def job_bank(unit, name):
            number = jobs.numbers[unit.layer, unit.u, name]
            return four_banks[number % 4] if unit.u < 0 and name[0] != "r" else work_banks[number % 2]

        def wait_taken(eng, unit, name, back=0):
            parity, value = jobs.taken(unit, name, back)
            wait(eng, work_taken[parity], value)

        def taken(unit, name):
            return work_taken[jobs.taken(unit, name)[0]]

        block = ctx.enter_context(nc.Block())

        @block.sync
        def _(sp):
            def load_qkv(l, b, cols):
                s = qkv_loaded[l][b]
                sp.dma_start(w_q[l][b][:, :, :], wq_dram[l][:, :, cols]).then_inc(s, 16)
                for w, dram in ((w_k, (Wk1, Wk2)[l]), (w_v, (Wv1, Wv2)[l])):
                    if l == 0:
                        sp.dma_start(w[l][b][:, :, :],
                                     dram.rearrange("(c p) n -> p c n", p=P)[:, :, cols]).then_inc(s, 16)
                    else:
                        for c, rows in enumerate(cross_attn.key_rows):
                            sp.dma_start(w[l][b][0:rows, c, :], dram[c * P:c * P + rows, cols]).then_inc(s, 16)

            for g in range(4):
                sp.dma_start(x_sb[:, 4 * g:4 * g + 4, :], x_dram[:, 4 * g:4 * g + 4, :]).then_inc(x_loaded[g], 16)
            for n, (g, b) in enumerate(((g1, b1), (g2, b2), (g3, b3))):
                sp.dma_start(gains[:, n, :], g.rearrange("(c p) -> p c", p=P), allow_slow_non_contiguous=True).then_inc(vec_loaded, 16)
                sp.dma_start(shifts[:, n, :], b.rearrange("(c p) -> p c", p=P), allow_slow_non_contiguous=True).then_inc(vec_loaded, 16)
            for n, b in enumerate((bo1, bo2, bf)):
                sp.dma_start(bias_b[:, n, :], b.partition_broadcast(P)).then_inc(vec_loaded, 16)
            sp.dma_start(bp_sb[:, :], bp.rearrange("(f p) -> p f", p=P), allow_slow_non_contiguous=True).then_inc(vec_loaded, 16)
            load_qkv(0, 0, slice(0, P))
            whole = CTX_TILES - 1
            for part, first, last in ((0, 0, STAGED), (1, STAGED, whole)):
                sp.dma_start(ctx_stage[part][:, 0:last - first, :],
                             ctx_rows[first * P:last * P, :].rearrange("(t p) d -> p t d", p=P)).then_inc(ctx_loaded, 16)
            sp.dma_start(ctx_tile(whole)[0:CTX_LAST, :], ctx_rows[whole * P:CTX_TOKENS, :]).then_inc(ctx_loaded, 16)
            def attention(l, A):
                def job(unit, name):
                    nxt = unit.next
                    if name == "q":
                        sp.wait_ge(hi_ready, jobs.split(unit, name) + 1)
                        for a in range(2):
                            q = q_hi[nxt % 2][a]
                            sp.dma_start(q[HALF:P, :].bitcast(FP32), q[0:HALF, :].bitcast(FP32)).then_inc(queries_doubled, 16)
                    elif name[0] == "k":
                        sp.wait_ge(hi_ready, jobs.split(unit, name) + 1)
                        start, width = layers[unit.next_pair_layer].key_chunks[int(name[1])]
                        b = unit.next_pair % 2
                        for a in range(2):
                            sp.dma_start(k_hi_one[b][a][0:HALF, start:start + width].bitcast(FP32),
                                         k_hi_lo[b][a][0:HALF, start:start + width].bitcast(FP32)).then_inc(keys_doubled, 16)
                    elif name[:3] == "row":
                        a = int(name[3])
                        wait_taken(sp, unit, name)
                        for i in range(Q_TILES):
                            sp.dma_start(q_lo[nxt % 2][a][HALF:HALF + 1, i * P:(i + 1) * P].bitcast(FP32),
                                         max_rows[a][i:i + 1, :].bitcast(FP32)).then_inc(rows_placed[a], 16)

                if l == 0:
                    for name in ("k0", "k1", "k2", "k3", "q"):
                        job(Unit(0, -1), name)
                    sp.wait_ge(consts_set, 1)
                    for b in range(2):
                        for a in range(2):
                            for n in range(TOKENS // BANK):
                                sp.dma_start(k_hi_one[b][a][HALF:HALF + 1, n * BANK:(n + 1) * BANK].bitcast(FP32),
                                             one_row[:, :]).then_inc(key_ones, 16)
                    for name in ("row0", "row1"):
                        job(Unit(0, -1), name)
                    load_qkv(0, 1, slice(P, 2 * P))
                    for layer in range(2):
                        for b in range(2):
                            sp.dma_start(w_o[layer][b][:, :], wo_dram[layer][:, b, :]).then_inc(wo_loaded[layer][b], 16)
                    for b in range(2):
                        load_qkv(1, b, slice(b * P, b * P + P))
                for unit in units(sp, l):
                    if l == 1 and unit.u == UNITS - CHUNKS:
                        sp.wait_ge(scores_ready[1], 2 * unit.u * A.steps)
                        sp.dma_start(w_p[:, :, :], Wp.rearrange("(c p) n -> p c n", p=P)).then_inc(ff_loaded, 16)
                        sp.dma_start(w_f[:, :, :], Wf.rearrange("(f p) n -> p f n", p=P)).then_inc(ff_loaded, 16)
                    for t in range(A.steps):
                        for name in A.jobs_at(unit, t):
                            job(unit, name)
                            if name == "q" and unit.chunk == 2 and unit.u // CHUNKS + 2 < PAIRS:
                                sp.wait_ge(work_ready, jobs.number(unit, "q") + 1)
                                b = unit.pair_parity
                                load_qkv(l, b, bass.ds(unit.at((unit.u // CHUNKS + 2) * P, 2 * P), P))
                            if name == "y1" and unit.chunk == 0 and CHUNKS <= unit.u < UNITS - CHUNKS:
                                sp.wait_ge(work_ready, jobs.number(unit, "y1") + 1)
                                pair = unit.u // CHUNKS + 1
                                sp.dma_start(w_o[l][pair % 2][:, :], wo_dram[l][:, bass.ds(unit.at(pair, 2), 1), :]
                                             .rearrange("p r n -> p (r n)")).then_inc(wo_loaded[l][pair % 2], 16)

            for l, A in enumerate(layers):
                attention(l, A)
            with sp.Fori(0, 2 * CHUNKS) as h:
                sp.wait_ge(result_ready, h + 1)
                sp.dma_start(out_dram[:, bass.ds(h * 2, 2), :], x_sb[:, bass.ds(h * 2, 2), :]).then_inc(out_stored, 16)
            sp.wait_ge(out_stored, 16 * 2 * CHUNKS)

        @block.gpsimd
        def _(pool):
            nc.gpsimd.memset(ident[:, :], 0.0).then_inc(ident_zeroed, 1)
            pool.wait_ge(ident_zeroed, 1)
            nc.gpsimd.affine_select(out=ident[:, :], in_=ident[:, :], compare_op=ALU.not_equal, fill=1.0,
                                    base=0, pattern=[[-1, P]], channel_multiplier=1).then_inc(ident_ready, 1)

            def attention(l, A):
                for unit in units(pool, l):
                    for s in range(1, A.steps):
                        rows = A.tile_keys[s]
                        acc = sums[0:rows, unit.parity, :, :]
                        first = probs[0:rows, unit.u * A.steps % RING, :, :] if s == 1 else acc
                        if s == 1 and not unit.first:
                            pool.wait_ge(work_ready, jobs.sums_read(unit))
                        if s > 1:
                            pool.wait_ge(sums_added[l], A.added(unit, s - 1))
                        pool.wait_ge(probs_ready[l], unit.at(2 * (unit.u * A.steps + s) + 2, 2 * PERIOD * A.steps))
                        nc.gpsimd.tensor_tensor(acc, first, probs[0:rows, (unit.u * A.steps + s) % RING, :, :],
                                                ALU.add).then_inc(sums_added[l], 1)

            attention(0, self_attn)
            attention(1, cross_attn)

        @block.tensor
        def _(pe):
            def turn_tokens(g):
                for c in range(DIM_TILES):
                    k = 2 * g + c
                    wait(pe, xn_ready, k - 3)
                    for j in range(4):
                        pe.wait_ge(normalised, 4 * g + j + 1)
                        last = nc.tensor.transpose(ff_banks[k % 4][:, j * P:(j + 1) * P],
                                                   xn_stage[:, 4 * g + j, c * P:(c + 1) * P], ident[:, :])
                    last.then_inc(xn_turned, 1)

            def turn_context(k):
                g, c = k // 2, k % 2
                rows = cross_attn.key_rows[c]
                wait(pe, ctx_ready, k)
                for t in range(4 * g, min(4 * g + 4, CTX_TILES)):
                    m = cross_attn.tile_keys[t]
                    last = nc.tensor.transpose(out_bank[0:rows, (t - 4 * g) * P:(t - 4 * g) * P + m],
                                               ctx_tile(t)[0:m, c * P:c * P + rows], ident[0:m, 0:m])
                last.then_inc(ctx_turned, 1)

            def attention(l, A):
                def scores(unit, t):
                    m = A.tile_keys[t]
                    cols = slice(t * P, t * P + m)
                    for a in range(2):
                        k_both, k_one = k_hi_lo[unit.pair_parity][a], k_hi_one[unit.pair_parity][a]
                        dst = score_banks[a][0:m, :]
                        if l == 1 and unit.u == 0 and t == 0:
                            pe.wait_ge(probs_ready[0], 2 * (UNITS * self_attn.steps - 1) + a + 1)
                        elif not (unit.first and t == 0):
                            pe.wait_ge(probs_ready[l], unit.at(2 * (unit.u * A.steps + t - 1) + a + 1,
                                                               2 * PERIOD * A.steps))
                        nc.tensor.matmul(dst, k_both[:, cols], q_hi[unit.parity][a][:, :], start=True, stop=False)
                        if t == 0:
                            pe.wait_ge(rows_placed[a], unit.at(64 * (unit.overall + 1), 64 * PERIOD))
                            if unit.chunk == 0 and a == 0:
                                pe.wait_ge(keys_doubled, unit.at(128 * (unit.overall // CHUNKS + 1), 256))
                        nc.tensor.matmul(dst, k_one[:, cols], q_lo[unit.parity][a][:, :],
                                         start=False, stop=True).then_inc(scores_ready[l], 1)
                        yield

                def weighted_values(unit, t):
                    m = A.tile_keys[t]
                    slot = (unit.u * A.steps + t) % RING
                    pe.wait_ge(probs_ready[l], unit.at(2 * (unit.u * A.steps + t) + 2, 2 * PERIOD * A.steps))
                    if t == 0 and not unit.first:
                        pe.wait_ge(out_copied, unit.at(unit.overall, PERIOD))
                        if unit.chunk == 0:
                            before = Unit(l, unit.u - 1, unit.i) if unit.u > 0 else Unit(0, UNITS - 1)
                            wait_taken(pe, before, "v3")
                    for a in range(2):
                        last = nc.tensor.matmul(out_bank[a * HALF:(a + 1) * HALF, :],
                                                v_sb[0:m, unit.pair_parity, t, a * HALF:(a + 1) * HALF],
                                                probs[0:m, slot, a, :], start=(t == 0), stop=(t == A.steps - 1))
                    last.then_inc(values_used[l], 1)

                def max_tile(unit, n):
                    nxt = unit.next
                    a, i, kc = n // 16, n // 4 % 4, n % 4
                    start, width = layers[unit.next_layer].max_chunks[kc]
                    dst = max_banks[n % 3][:, 0:width]
                    last_in_bank = n - 3 if n > 2 else MAX_TILES - 1 - (MAX_TILES - 1 - n) % 3 - MAX_TILES
                    if not (unit.u == -1 and n < 3):
                        pe.wait_ge(max_tile_taken, unit.at(MAX_TILES * (unit.overall + 1) + last_in_bank + 1,
                                                           PERIOD * MAX_TILES))
                    if n == 0:
                        wait_taken(pe, unit, "q")
                        pe.wait_ge(queries_doubled, unit.at(32 * (unit.overall + 2), 32 * PERIOD))
                    nc.tensor.matmul(dst, q_hi[nxt % 2][a][:, i * P:(i + 1) * P],
                                     k_hi_lo[(nxt // CHUNKS) % 2][a][:, start:start + width],
                                     start=True, stop=True).then_inc(max_tile_ready, 1)

                def job(unit, name):
                    work = job_bank(unit, name)
                    wait_taken(pe, unit, name, 4 if unit.u < 0 and name[0] in "kq" else 2)
                    nxt, pair = unit.next, unit.next_pair
                    B = layers[unit.next_pair_layer]
                    src = (xn_t, ctx_t)[B.layer]
                    if name == "q":
                        chunk = nxt % CHUNKS
                        for c in range(DIM_TILES):
                            last = nc.tensor.matmul(work[:, :], w_q[unit.next_layer][(nxt // CHUNKS) % 2][:, c, :],
                                                    xn_t[:, c, chunk * BANK:(chunk + 1) * BANK],
                                                    start=(c == 0), stop=(c == DIM_TILES - 1))
                    elif name[0] == "k":
                        if name == "k0":
                            pe.wait_ge(qkv_loaded[B.layer][pair % 2],
                                       unit.at(16 * QKV_DMAS[B.layer] * (pair // 2 + 1), 16 * QKV_DMAS[B.layer]))
                        start, width = B.key_chunks[int(name[1])]
                        for c, rows in enumerate(B.key_rows):
                            last = nc.tensor.matmul(work[:, 0:width], w_k[B.layer][pair % 2][0:rows, c, :],
                                                    src[0:rows, c, start:start + width],
                                                    start=(c == 0), stop=(c == DIM_TILES - 1))
                    elif name[0] == "v":
                        for t in range(4 * int(name[1]), min(4 * int(name[1]) + 4, B.steps)):
                            m = B.tile_keys[t]
                            for c, rows in enumerate(B.key_rows):
                                last = nc.tensor.matmul(work[0:m, (t % 4) * P:(t % 4 + 1) * P],
                                                        src[0:rows, c, t * P:t * P + m],
                                                        w_v[B.layer][pair % 2][0:rows, c, :],
                                                        start=(c == 0), stop=(c == DIM_TILES - 1))
                    elif name == "sum":
                        if unit.prev_layer == l:
                            pe.wait_ge(sums_added[l], unit.at(unit.u * A.adds, PERIOD * A.adds))
                        else:
                            pe.wait_ge(sums_added[0], UNITS * self_attn.adds)
                        prev = (unit.u - 1) % 2
                        for a in range(2):
                            last = nc.tensor.matmul(work[a * HALF:(a + 1) * HALF, :], ones[:, 0:HALF],
                                                    sums[:, prev, a, :], start=True, stop=True)
                    elif name[0] == "y":
                        prev_pair = unit.prev_pair
                        if name == "y0":
                            pe.wait_ge(out_normed, unit.at(unit.overall, PERIOD))
                            if (unit.u - 1) % CHUNKS == 0:
                                pe.wait_ge(wo_loaded[l][prev_pair % 2], unit.at(16 * (prev_pair // 2 + 1), 16))
                        for k in range(2):
                            i = 2 * int(name[1]) + k
                            last = nc.tensor.matmul(work[:, k * DIM:(k + 1) * DIM], o_norm[:, i * P:(i + 1) * P],
                                                    w_o[unit.prev_layer][prev_pair % 2][:, :], start=True, stop=True)
                    elif name[:2] == "ln":
                        norm, chunk = unit.norm(int(name[2]) // 2)
                        c = int(name[2]) % 2
                        pe.wait_ge(normalised, TOKEN_TILES * norm + 4 * chunk + 4)
                        for j in range(Q_TILES):
                            last = nc.tensor.transpose(work[:, j * P:(j + 1) * P],
                                                       norm_stage[:, j, c * P:(c + 1) * P], ident[:, :])
                    else:
                        a = int(name[3])
                        pe.wait_ge(head_max_ready, unit.at(2 * (unit.overall + 1) + a + 1, 2 * PERIOD))
                        last = nc.tensor.transpose(work[0:Q_TILES, 0:P],
                                                   query_max[:, a * Q_TILES:(a + 1) * Q_TILES], ident[:, :])
                    last.then_inc(work_ready, 1)

                if l == 0:
                    before = Unit(0, -1)
                    pe.wait_ge(ident_ready, 1)
                    for g in range(CHUNKS):
                        turn_tokens(g)
                        if g > 0:
                            pe.wait_ge(xn_ready, 2 * g)
                            job(before, f"k{g - 1}")
                    pe.wait_ge(xn_ready, 8)
                    job(before, "k3")
                    job(before, "q")
                    job(before, "v0")
                    job(before, "v1")
                    pe.wait_ge(ctx_loaded, 48)
                    for n in range(MAX_TILES):
                        max_tile(before, n)
                        if n in (3, 7):
                            job(before, f"v{2 + n // 4}")
                        if n % 2 == 1 and 9 <= n < 25:
                            turn_context((n - 9) // 2)
                        if n == 19:
                            job(before, "row0")
                    job(before, "row1")
                    pe.wait_ge(consts_set, 1)
                    pe.wait_ge(key_ones, 16 * 4 * CHUNKS)
                    pe.wait_ge(ctx_ready, 8)
                for unit in units(pe, l):
                    for t in range(A.steps):
                        tiles = list(A.max_at[t]) if unit.has_next else []
                        for _ in scores(unit, t):
                            if tiles and tiles[0] > 0:
                                max_tile(unit, tiles.pop(0))
                        for name in A.jobs_at(unit, t):
                            job(unit, name)
                        if t > 0:
                            weighted_values(unit, t - 1)
                        elif unit.u > 0:
                            weighted_values(Unit(l, unit.u - 1, unit.i), A.steps - 1)
                        for n in tiles:
                            max_tile(unit, n)
                weighted_values(unit, A.steps - 1)
                return job

            attention(0, self_attn)
            job = attention(1, cross_attn)
            after = Unit(1, UNITS)
            job(after, "sum")

            pe.wait_ge(ff_loaded, 32)
            pe.wait_ge(max_tile_taken, 2 * UNITS * MAX_TILES)
            pe.wait_ge(probs_ready[1], 2 * UNITS * cross_attn.steps)
            pe.wait_ge(out_copied, 2 * UNITS)

            def feed_forward(q):
                for f in range(FF_TILES):
                    for name in {2: ("y0", "y1"), 5: ("ln0", "ln1")}.get(f, ()) if isinstance(q, int) else ():
                        job(after, name)
                    gate, up = ff_banks[2 * (f % 2)], ff_banks[2 * (f % 2) + 1]
                    wait(pe, hidden_done, q * FF_TILES + (f - 1))
                    for dst, col, s in ((gate, FF + f * P, gate_ready), (up, f * P, up_ready)):
                        for c in range(DIM_TILES):
                            last = nc.tensor.matmul(dst[:, :], w_p[:, c, col:col + P],
                                                    xn_t[:, c, bass.ds(q * BANK, BANK)],
                                                    start=(c == 0), stop=(c == DIM_TILES - 1))
                        last.then_inc(s, 1)
                for j in range(2):
                    wait(pe, result_ready, q * 2 + (j - 1))
                    for k in range(2):
                        i = 2 * j + k
                        for f in range(FF_TILES):
                            if i == 0:
                                pe.wait_ge(hidden_done, q * FF_TILES + f + 1)
                            last = nc.tensor.matmul(score_banks[j][:, k * DIM:(k + 1) * DIM],
                                                    hidden[:, f, i * P:(i + 1) * P], w_f[:, f, :],
                                                    start=(f == 0), stop=(f == FF_TILES - 1))
                    last.then_inc(down_ready, 1)

            feed_forward(0)
            for name in ("ln0", "ln1"):
                wait_taken(pe, after, name)
            with pe.Fori(1, CHUNKS) as q:
                feed_forward(q)

        @block.scalar
        def _(act):
            def std_of(n, g):
                act.wait_ge(moments_done, TOKEN_TILES * n + 4 * g + 4)
                nc.scalar.activation(std[:, 4 * g:4 * g + 4], moments[:, 4 * g:4 * g + 4, 1], ACT.Sqrt,
                                     bias=eps_col[:, :]).then_inc(std_done, 1)

            def take_norm(n, g, c, bank, done):
                nc.scalar.activation(xn_t[:, c, g * BANK:(g + 1) * BANK], bank[:, :], ACT.Identity,
                                     bias=shifts[:, n, c:c + 1], scale=gains[:, n, c:c + 1]).then_inc(done, 1)

            def take_first_norm(g):
                for c in range(DIM_TILES):
                    k = 2 * g + c
                    act.wait_ge(xn_turned, k + 1)
                    take_norm(0, g, c, ff_banks[k % 4], xn_ready)

            def take_context(k):
                g, c = k // 2, k % 2
                rows, width = cross_attn.key_rows[c], min(BANK, CTX_TOKENS - g * BANK)
                act.wait_ge(ctx_turned, k + 1)
                nc.scalar.copy(ctx_t[0:rows, c, g * BANK:g * BANK + width],
                               out_bank[0:rows, 0:width]).then_inc(ctx_ready, 1)

            def attention(l, A):
                def exp(unit, t):
                    m = A.tile_keys[t]
                    slot = (unit.u * A.steps + t) % RING
                    for a in range(2):
                        act.wait_ge(scores_ready[l], unit.at(2 * (unit.u * A.steps + t) + a + 1,
                                                             2 * PERIOD * A.steps))
                        if a == 0 and not (unit.first and t < RING):
                            if t >= RING:
                                act.wait_ge(values_used[l], unit.at(unit.u * A.steps + t - RING + 1, PERIOD * A.steps))
                                act.wait_ge(sums_added[l], A.added(unit, t - RING))
                            else:
                                B = layers[unit.prev_layer]
                                prev = Unit(B.layer, (unit.u - 1) % UNITS, unit.i)
                                act.wait_ge(values_used[B.layer], prev.at(prev.u * B.steps + B.steps + t - RING + 1,
                                                                          PERIOD * B.steps))
                                act.wait_ge(sums_added[B.layer], B.added(prev, B.steps + t - RING))
                        src = score_banks[a][0:m, :]
                        nc.scalar.activation(probs[0:m, slot, a, :], src, ACT.Exp,
                                             scale=SCALE).then_inc(probs_ready[l], 1)

                def job(unit, name):
                    if name[0] not in "qkvrl":
                        return
                    act.wait_ge(work_ready, jobs.number(unit, name) + 1)
                    work = job_bank(unit, name)
                    nxt, pair_parity = unit.next, unit.next_pair % 2
                    B = layers[unit.next_pair_layer]
                    if name == "q":
                        for a in range(2):
                            src = work[a * HALF:(a + 1) * HALF, :]
                            last = nc.scalar.copy(q_hi[nxt % 2][a][0:HALF, :], src)
                        last.then_inc(hi_ready, 1)
                    elif name[0] == "k":
                        start, width = B.key_chunks[int(name[1])]
                        for a in range(2):
                            src = work[a * HALF:(a + 1) * HALF, 0:width]
                            last = nc.scalar.copy(k_hi_lo[pair_parity][a][0:HALF, start:start + width], src)
                        last.then_inc(hi_ready, 1)
                    elif name[0] == "v":
                        t0 = 4 * int(name[1])
                        tiles = min(4, B.steps - t0)
                        m = B.tile_keys[t0]
                        nc.scalar.copy(v_sb[0:m, pair_parity, t0:t0 + tiles, :],
                                       work[0:m, 0:tiles * P].rearrange("p (t n) -> p t n", n=P)
                                       ).then_inc(taken(unit, name), 1)
                    elif name[:2] == "ln":
                        norm, chunk = unit.norm(int(name[2]) // 2)
                        take_norm(norm, chunk, int(name[2]) % 2, work, taken(unit, name))
                    else:
                        nc.scalar.mul(max_rows[int(name[3])][:, :], work[0:Q_TILES, 0:P],
                                      -1.0).then_inc(taken(unit, name), 1)

                def copy_out(unit):
                    if unit.prev_layer == l:
                        act.wait_ge(values_used[l], unit.at(unit.u * A.steps, PERIOD * A.steps))
                    else:
                        act.wait_ge(values_used[0], UNITS * self_attn.steps)
                    nc.scalar.copy(o_raw[:, (unit.u - 1) % 2, :], out_bank[:, :]).then_inc(out_copied, 1)

                if l == 0:
                    before = Unit(0, -1)
                    act.wait_ge(consts_set, 1)
                    for g in range(3):
                        std_of(0, g)
                    act.wait_ge(vec_loaded, 160)
                    take_first_norm(0)
                    std_of(0, 3)
                    for g in range(1, CHUNKS):
                        take_first_norm(g)
                        job(before, f"k{g - 1}")
                    for name in ("k3", "q", "v0", "v1", "v2", "v3"):
                        job(before, name)
                    for k in range(6):
                        take_context(k)
                    job(before, "row0")
                    for k in range(6, 8):
                        take_context(k)
                    job(before, "row1")
                for unit in units(act, l):
                    for t in range(A.steps):
                        exp(unit, t)
                        for half, step in enumerate((1, A.steps - 2)):
                            if t == step and unit.norm(half):
                                std_of(*unit.norm(half))
                        for name in A.jobs_at(unit, t):
                            job(unit, name)
                        if t == 0 and not unit.first:
                            copy_out(unit)
                return job, copy_out

            attention(0, self_attn)
            job, copy_out = attention(1, cross_attn)
            after = Unit(1, UNITS)
            copy_out(after)

            def gelu(q):
                for f in range(FF_TILES):
                    if isinstance(q, int) and f == 3:
                        std_of(*after.norm(0))
                    if isinstance(q, int) and f == 5:
                        job(after, "ln0")
                        job(after, "ln1")
                    wait(act, gate_ready, q * FF_TILES + (f + 1))
                    wait(act, hidden_done, q * FF_TILES + (f - 1))
                    nc.scalar.activation(gelu_sb[:, f % 2, :], ff_banks[2 * (f % 2)][:, :], ACT.Gelu,
                                         bias=bp_sb[:, FF_TILES + f:FF_TILES + f + 1]).then_inc(gelu_done, 1)

            gelu(0)
            with act.Fori(1, CHUNKS) as q:
                gelu(q)

        @block.vector
        def _(dve):
            nc.vector.memset(ones[:, :], 1.0)
            nc.vector.memset(one_row[:, :], 1.0)
            nc.vector.memset(eps_col[:, :], EPS).then_inc(consts_set, 1)

            def token_stats(n, g):
                for t in range(4 * g, 4 * g + 4):
                    nc.vector.bn_stats(stats[:, t, :], x_sb[:, t, :]).then_inc(stats_done, 1)
                for t in range(4 * g, 4 * g + 4):
                    dve.wait_ge(stats_done, TOKEN_TILES * n + t + 1)
                    nc.vector.bn_aggr(moments[:, t, :], stats[:, t, :]).then_inc(moments_done, 1)

            def normalise(n, g, stage):
                dve.wait_ge(std_done, 4 * n + g + 1)
                nc.vector.reciprocal(rstd[:, 4 * g:4 * g + 4], std[:, 4 * g:4 * g + 4]).then_inc(rstd_done, 1)
                dve.wait_ge(rstd_done, 4 * n + g + 1)
                for j in range(4):
                    t = 4 * g + j
                    nc.vector.tensor_scalar(stage[:, j, :], x_sb[:, t, :], moments[:, t, 0:1],
                                            rstd[:, t:t + 1], ALU.subtract, ALU.mult).then_inc(normalised, 1)

            def add_bias(n, g):
                dve.wait_ge(normalised, TOKEN_TILES * n + 4 * g + 4)
                rows = x_sb[:, 4 * g:4 * g + 4, :]
                nc.vector.tensor_tensor(rows, rows, bias_b[:, n:n + 1, :].to_broadcast([P, 4, DIM]),
                                        ALU.add).then_inc(bias_added, 1)

            def first_norm():
                for g in range(CHUNKS + 1):
                    if g < CHUNKS:
                        dve.wait_ge(x_loaded[g], 16)
                        token_stats(0, g)
                    if g > 0:
                        normalise(0, g - 1, xn_stage[:, 4 * g - 4:4 * g, :])

            def later_stats(unit, half):
                n, g = unit.norm(half)
                from_unit = unit if half == 1 or unit.u == UNITS else Unit(*((unit.layer, unit.u - 1) if unit.u > 0
                                                                             else (0, UNITS - 1)))
                wait_taken(dve, from_unit, "y1")
                token_stats(n, g)

            def later_norm(unit, half):
                n, g = unit.norm(half)
                if (n, g) != (1, 0):
                    dve.wait_ge(work_ready, jobs.last_turned(unit, half))
                normalise(n, g, norm_stage)
                add_bias(n, g)

            def attention(l, A):
                def take_max(unit, n):
                    nxt = unit.overall + 1
                    a, j, kc = n // 16, n // 4, n % 4
                    width = layers[unit.next_layer].max_chunks[kc][1]
                    dve.wait_ge(max_tile_ready, unit.at(MAX_TILES * nxt + n + 1, PERIOD * MAX_TILES))
                    nc.vector.tensor_reduce(part_max[:, j, kc:kc + 1], max_banks[n % 3][:, 0:width], AX.X,
                                            ALU.max).then_inc(max_tile_taken, 1)
                    if n % 16 == 15:
                        dve.wait_ge(max_tile_taken, unit.at(MAX_TILES * nxt + n + 1, PERIOD * MAX_TILES))
                        heads = slice(a * Q_TILES, (a + 1) * Q_TILES)
                        nc.vector.tensor_reduce(query_max[:, heads], part_max[:, heads, :], AX.X,
                                                ALU.max).then_inc(head_max_ready, 1)

                def job(unit, name):
                    nxt = unit.next
                    work = job_bank(unit, name)
                    if name[0] in "qk":
                        pair_parity = unit.next_pair % 2
                        dve.wait_ge(hi_ready, jobs.split(unit, name) + 1)
                        for a in range(2):
                            if name == "q":
                                hi = q_hi[nxt % 2][a][0:HALF, :]
                                lo, width = q_lo[nxt % 2][a][0:HALF, :], BANK
                            else:
                                start, width = layers[unit.next_pair_layer].key_chunks[int(name[1])]
                                both = k_hi_lo[pair_parity][a]
                                hi, lo = both[0:HALF, start:start + width], both[HALF:P, start:start + width]
                            last = nc.vector.tensor_tensor(lo, work[a * HALF:(a + 1) * HALF, 0:width],
                                                           hi.bitcast(FP32), ALU.subtract)
                        last.then_inc(taken(unit, name), 1)
                    elif name == "sum":
                        dve.wait_ge(work_ready, jobs.number(unit, name) + 1)
                        for part in range(4):
                            cols = slice(part * P, (part + 1) * P)
                            last = nc.vector.reciprocal(sum_recip[:, cols], work[:, cols])
                            if part < 3:
                                yield
                        last.then_inc(taken(unit, name), 1)
                        wait_taken(dve, unit, name)
                        dve.wait_ge(out_copied, unit.at(unit.overall, PERIOD))
                        nc.vector.tensor_tensor(o_norm[:, :], o_raw[:, (unit.u - 1) % 2, :], sum_recip[:, :],
                                                ALU.mult).then_inc(out_normed, 1)
                    elif name[0] == "y":
                        t = 4 * ((unit.u - 1) % CHUNKS) + 2 * int(name[1])
                        rows = x_sb[:, t:t + 2, :]
                        dve.wait_ge(work_ready, jobs.number(unit, name) + 1)
                        nc.vector.tensor_tensor(rows, rows, work[:, :].rearrange("p (t d) -> p t d", d=DIM),
                                                ALU.add).then_inc(taken(unit, name), 1)

                def finish(parts):
                    for _ in parts:
                        pass

                if l == 0:
                    before = Unit(0, -1)
                    for name in ("k0", "k1", "k2", "k3", "q"):
                        finish(job(before, name))
                    for n in range(MAX_TILES):
                        take_max(before, n)
                    dve.wait_ge(vec_loaded, 160)
                    for g in range(CHUNKS):
                        add_bias(0, g)
                late_keys = None
                for unit in units(dve, l):
                    if unit.u == 1:
                        dve.wait_ge(bias_added, 4 * l + 4)
                    for t in range(A.steps):
                        tiles = list(A.max_at[t]) if unit.has_next else []
                        for half, step in enumerate((1, A.steps - 2)):
                            if unit.norm(half) and t == step:
                                later_stats(unit, half)
                                if half == 0:
                                    later_norm(unit, half)
                            if unit.norm(half) and half == 1 and t == step + 1:
                                later_norm(unit, half)
                        if late_keys:
                            finish(job(unit, late_keys))
                            late_keys = None
                        for _ in range(A.recips_at(unit, t)):
                            next(recips, None)
                        for n in tiles:
                            take_max(unit, n)
                        for name in A.jobs_at(unit, t):
                            if name[0] == "k" and t < A.steps - 1:
                                late_keys = name
                            elif name == "sum":
                                recips = job(unit, name)
                            else:
                                finish(job(unit, name))
                return job

            first_norm()
            attention(0, self_attn)
            job = attention(1, cross_attn)
            after = Unit(1, UNITS)
            for _ in job(after, "sum"):
                pass

            def feed_forward(q):
                for f in range(FF_TILES):
                    if isinstance(q, int) and f == 2:
                        for name in ("y0", "y1"):
                            list(job(after, name))
                        later_stats(after, 0)
                    if isinstance(q, int) and f == 3:
                        later_norm(after, 0)
                    dve.wait_ge(up_ready, q * FF_TILES + (f + 1))
                    dve.wait_ge(gelu_done, q * FF_TILES + (f + 1))
                    wait(dve, down_ready, q * 2)
                    nc.vector.scalar_tensor_tensor(hidden[:, f, :], ff_banks[2 * (f % 2) + 1][:, :],
                                                   bp_sb[:, f:f + 1], gelu_sb[:, f % 2, :], ALU.add,
                                                   ALU.mult).then_inc(hidden_done, 1)
                for j in range(2):
                    dve.wait_ge(down_ready, q * 2 + (j + 1))
                    if isinstance(q, int):
                        dve.wait_ge(bias_added, 12)
                    rows = x_sb[:, bass.ds(q * 4 + 2 * j, 2), :]
                    nc.vector.tensor_tensor(rows, rows, score_banks[j][:, :].rearrange("p (t d) -> p t d", d=DIM),
                                            ALU.add).then_inc(result_ready, 1)

            feed_forward(0)
            with dve.Fori(1, CHUNKS) as q:
                feed_forward(q)


_PREFIX = "L0_xattn_"
_NAMES = ["Wq1", "Wk1", "Wv1", "Wo1", "bo1", "Wq2", "Wk2", "Wv2", "Wo2", "bo2", "Wp", "bp", "Wf", "bf",
          "g1", "b1", "g2", "b2", "g3", "b3"]
_INS = ["x", "ctx_768"] + [_PREFIX + n for n in _NAMES]


def kernel(**inputs):
    import numpy as _np
    import concourse.bacc as _bacc
    from concourse import mybir as _mybir
    from concourse.bass_utils import run_bass_kernel_spmd as _run

    nc = _bacc.Bacc("TRN2", target_bir_lowering=False, num_devices=1)
    arrays, args = {}, []
    for name in _INS:
        a = _np.ascontiguousarray(inputs[name])
        arrays[f"in_{name}_dram"] = a
        args.append(nc.dram_tensor(f"in_{name}_dram", a.shape, _mybir.dt.from_np(a.dtype), kind="ExternalInput").ap())
    out = nc.dram_tensor("out_dram", (1, TOKENS, DIM), _mybir.dt.float32, kind="ExternalOutput").ap()
    xattn_block(nc, *args, out)
    r = _run(nc, [arrays], core_ids=[0])
    return r.results[0]["out_dram"]
```
